# Optimizing a Trainium2 kernel written in Bass

```python
import numpy as np
import jax
import jax.numpy as jnp

def _softmax(x, axis=-1):
    return jax.nn.softmax(x, axis=axis)

def _gelu(x):
    return jax.nn.gelu(x, approximate=True)

def _silu(x):
    return jax.nn.silu(x)

def _sigmoid(x):
    return jax.nn.sigmoid(x)

def _layernorm(x, axis=-1, eps=1e-05):
    m = jnp.mean(x, axis=axis, keepdims=True)
    v = jnp.var(x, axis=axis, keepdims=True)
    return (x - m) / jnp.sqrt(v + eps)

def _scatter_add(tgt, idx, src, axis=0):
    return tgt.at[idx].add(src)

def _segment_sum(src, seg, n):
    return jax.ops.segment_sum(src, seg, n)
kernel_name = 'mk_xattn_ffn_d4_seqx_r8_a664a6'

def setup_inputs(seed: int=0):
    np.random.seed(seed)
    _w = jnp.asarray

    def _rec_inputs():
        import jax
        import jax.numpy as jnp
        _rk = jax.random.key(seed)
        x = -0.0002928 + 1 * jax.random.normal(jax.random.fold_in(_rk, 1), (8, 128, 128), jnp.float32)
        _lenS = 128 - jax.random.randint(jax.random.fold_in(_rk, 7), (8,), 0, max(1, 128 // 4) + 1, jnp.int32)
        _lenS2 = 128 - jax.random.randint(jax.random.fold_in(_rk, 8), (8,), 0, max(1, 128 // 4) + 1, jnp.int32)
        _ctx_1024P = jax.random.normal(jax.random.fold_in(_rk, 11), (8, 16, 128), jnp.float32)
        _ctx_1024c = jax.random.dirichlet(jax.random.fold_in(_rk, 511), 0.3 * jnp.ones((16,), jnp.float32), (8, 128))
        _ctx_1024t = jnp.einsum('bsk,bkd->bsd', _ctx_1024c, _ctx_1024P)
        _ctx_1024t = _ctx_1024t * jax.lax.rsqrt(jnp.mean(jnp.square(_ctx_1024t)) + 1e-12) * 0.953939
        ctx_1024 = -1.39393e-06 + 0.999914 * (_ctx_1024t + 0.3 * jax.random.normal(jax.random.fold_in(_rk, 611), (8, 128, 128), jnp.float32))
        _validS = jnp.arange(128)[None, :] < _lenS[:, None]
        _validS2 = jnp.arange(128)[None, :] < _lenS2[:, None]
        _causal = jnp.tril(jnp.ones((128, 128), dtype=bool))
        mask_Bx1xSxS2_bk0 = jnp.logical_not(jnp.broadcast_to(_validS2[:, None, None, :], (8, 1, 128, 128)))
        return (x, ctx_1024, mask_Bx1xSxS2_bk0)
    x, ctx_1024, mask_Bx1xSxS2_bk0 = _rec_inputs()

    def _L0_xattn_setup():
        import jax, jax.numpy as jnp
        import numpy as np
        NUM_HEADS = 16
        D_MODEL = 128
        NEG_INF = -1e+30

        def _split_heads(x, h):
            B, S, D = x.shape
            return x.reshape(B, S, h, D // h).transpose(0, 2, 1, 3)
        key = jax.random.key(seed)
        ks = jax.random.split(key, 7)
        B, S, D = (2, 256, D_MODEL)
        scale = 1.0 / np.sqrt(D)
        return {'queries': jax.random.normal(ks[0], (B, S, D), dtype=jnp.float32), 'keys': jax.random.normal(ks[1], (B, S, D), dtype=jnp.float32), 'values': jax.random.normal(ks[2], (B, S, D), dtype=jnp.float32), 'Wq': jax.random.normal(ks[3], (D, D), dtype=jnp.float32) * scale, 'Wk': jax.random.normal(ks[4], (D, D), dtype=jnp.float32) * scale, 'Wv': jax.random.normal(ks[5], (D, D), dtype=jnp.float32) * scale, 'Wo': jax.random.normal(ks[6], (D, D), dtype=jnp.float32) * scale}
    _L0_xattn_all = _L0_xattn_setup()
    _L0_xattn_in = {k: v for k, v in _L0_xattn_all.items() if k in ('Wq', 'Wk', 'Wv', 'Wo')}
    del _L0_xattn_all

    def _L0_ffn_setup():
        import jax, jax.numpy as jnp
        import numpy as np
        CAPACITY_FACTOR = 1.0
        key = jax.random.key(seed)
        ks = jax.random.split(key, 5)
        B, S, D, E, F = (2, 256, 128, 8, 512)
        x = jax.random.normal(ks[0], (B, S, D), dtype=jnp.float32)
        Ws = jax.random.normal(ks[1], (D, E), dtype=jnp.float32) * (1.0 / np.sqrt(D))
        bs = jnp.zeros((E,), dtype=jnp.float32)
        W1 = jax.random.normal(ks[2], (E, D, F), dtype=jnp.float32) * (1.0 / np.sqrt(D))
        b1 = jnp.zeros((E, F), dtype=jnp.float32)
        W2 = jax.random.normal(ks[3], (E, F, D), dtype=jnp.float32) * (1.0 / np.sqrt(F))
        b2 = jnp.zeros((E, D), dtype=jnp.float32)
        return {'x': x, 'Ws': Ws, 'bs': bs, 'W1': W1, 'b1': b1, 'W2': W2, 'b2': b2}
    _L0_ffn_all = _L0_ffn_setup()
    _L0_ffn_in = {k: v for k, v in _L0_ffn_all.items() if k in ('Ws', 'bs', 'W1', 'b1', 'W2', 'b2')}
    del _L0_ffn_all

    def _L1_xattn_setup():
        import jax, jax.numpy as jnp
        import numpy as np
        D_MODEL = 128
        N_HEADS = 16
        D_HEAD = D_MODEL // N_HEADS
        B = 4
        S = 256
        NEG_INF = -10000000000.0
        key = jax.random.key(seed)
        ks = jax.random.split(key, 8)
        queries = jax.random.normal(ks[0], (B, S, D_MODEL), dtype=jnp.float32)
        keys = jax.random.normal(ks[1], (B, S, D_MODEL), dtype=jnp.float32)
        values = jax.random.normal(ks[2], (B, S, D_MODEL), dtype=jnp.float32)
        causal = jnp.tril(jnp.ones((S, S), dtype=bool))
        mask = jnp.broadcast_to(causal[None, None, :, :], (B, 1, S, S))
        sc = 1.0 / np.sqrt(D_MODEL)
        W_q = jax.random.normal(ks[3], (D_MODEL, D_MODEL), dtype=jnp.float32) * sc
        W_k = jax.random.normal(ks[4], (D_MODEL, D_MODEL), dtype=jnp.float32) * sc
        W_v = jax.random.normal(ks[5], (D_MODEL, D_MODEL), dtype=jnp.float32) * sc
        W_proj = jax.random.normal(ks[6], (D_MODEL, D_MODEL), dtype=jnp.float32) * sc
        b_proj = jnp.zeros((D_MODEL,), dtype=jnp.float32)
        return {'queries': queries, 'keys': keys, 'values': values, 'mask': mask, 'W_q': W_q, 'W_k': W_k, 'W_v': W_v, 'W_proj': W_proj, 'b_proj': b_proj}
    _L1_xattn_all = _L1_xattn_setup()
    _L1_xattn_in = {k: v for k, v in _L1_xattn_all.items() if k in ('W_q', 'W_k', 'W_v', 'W_proj', 'b_proj')}
    del _L1_xattn_all

    def _L1_ffn_setup():
        import jax, jax.numpy as jnp
        import numpy as np
        BLOCK = 32
        W_BITS = 4
        ACT_BITS = 16

        def act_qdq(x):
            qmax = 2.0 ** (ACT_BITS - 1) - 1.0
            scale = jnp.maximum(jnp.max(jnp.abs(x)) / qmax, 1e-12)
            return jnp.clip(jnp.round(x / scale), -qmax - 1.0, qmax) * scale

        def fixed_qdq_u16(x):
            scale = 1.0 / 65536.0
            return jnp.clip(jnp.round(x / scale), 0.0, 65535.0) * scale

        def lpbq_dequant(w):
            O, I = w.shape
            qmax = 2.0 ** (W_BITS - 1) - 1.0
            wb = w.reshape(O, I // BLOCK, BLOCK)
            s = jnp.maximum(jnp.max(jnp.abs(wb), axis=-1, keepdims=True) / qmax, 1e-12)
            wq = jnp.clip(jnp.round(wb / s), -qmax - 1.0, qmax) * s
            return wq.reshape(O, I)
        key = jax.random.key(seed)
        k1, k2, k3, k4 = jax.random.split(key, 4)
        B, S, H, I = (2, 512, 128, 384)
        x = jax.random.normal(k1, (B, S, H), jnp.float32)
        w_gate = jax.random.normal(k2, (I, H), jnp.float32) * 0.02
        w_up = jax.random.normal(k3, (I, H), jnp.float32) * 0.02
        w_down = jax.random.normal(k4, (H, I), jnp.float32) * 0.02
        return {'x': x, 'w_gate': w_gate, 'w_up': w_up, 'w_down': w_down}
    _L1_ffn_all = _L1_ffn_setup()
    _L1_ffn_in = {k: v for k, v in _L1_ffn_all.items() if k in ('w_gate', 'w_up', 'w_down')}
    del _L1_ffn_all

    def _L2_xattn_setup():
        import jax, jax.numpy as jnp
        import numpy as np
        B, SQ, SK, D, H = (4, 256, 256, 128, 16)
        HD = D // H
        key = jax.random.key(seed)
        ks = jax.random.split(key, 8)
        s = 1.0 / np.sqrt(D)
        return {'query': jax.random.normal(ks[0], (B, SQ, D), jnp.float32), 'key_value': jax.random.normal(ks[1], (B, SK, D), jnp.float32), 'Wq': jax.random.normal(ks[2], (D, D), jnp.float32) * s, 'bq': jnp.zeros((D,), jnp.float32), 'Wkv': jax.random.normal(ks[3], (D, 2 * D), jnp.float32) * s, 'bkv': jnp.zeros((2 * D,), jnp.float32), 'Wo': jax.random.normal(ks[4], (D, D), jnp.float32) * s, 'bo': jnp.zeros((D,), jnp.float32)}
    _L2_xattn_all = _L2_xattn_setup()
    _L2_xattn_in = {k: v for k, v in _L2_xattn_all.items() if k in ('Wq', 'bq', 'Wkv', 'bkv', 'Wo', 'bo')}
    del _L2_xattn_all

    def _L2_ffn_setup():
        import jax, jax.numpy as jnp
        import numpy as np
        E = 8
        D = 128
        F = 512
        S, B = (256, 2)
        LN_EPS = 1e-05

        def _moe_forward(input_features, centroids, ln_g, ln_b, W1, b1, W2, b2):
            s, b, d = input_features.shape
            x = jnp.swapaxes(input_features, 0, 1).reshape(-1, d)
            logits = x.astype(jnp.float32) @ centroids.astype(jnp.float32).T
            assign = jnp.argmax(logits, axis=-1)
            onehot = jax.nn.one_hot(assign, E, dtype=x.dtype)
            disp = jnp.einsum('te,td->etd', onehot, x)
            mu = disp.mean(-1, keepdims=True)
            var = disp.var(-1, keepdims=True)
            xn = (disp - mu) * jax.lax.rsqrt(var + LN_EPS)
            xn = xn * ln_g[:, None, :] + ln_b[:, None, :]
            h = jax.nn.relu(jnp.einsum('etd,edf->etf', xn, W1) + b1[:, None, :])
            y = jnp.einsum('etf,efd->etd', h, W2) + b2[:, None, :]
            y = disp + y
            out = jnp.einsum('te,etd->td', onehot, y)
            return jnp.swapaxes(out.reshape(b, s, d), 0, 1)
        key = jax.random.key(seed)
        ks = jax.random.split(key, 8)
        scale_in = 1.0 / np.sqrt(D)
        scale_ff = 1.0 / np.sqrt(F)
        return {'input_features': jax.random.normal(ks[0], (S, B, D), dtype=jnp.float32), 'centroids': jax.random.normal(ks[1], (E, D), dtype=jnp.float32) * scale_in, 'ln_g': jnp.ones((E, D), dtype=jnp.float32), 'ln_b': jnp.zeros((E, D), dtype=jnp.float32), 'W1': jax.random.normal(ks[2], (E, D, F), dtype=jnp.float32) * scale_in, 'b1': jax.random.normal(ks[3], (E, F), dtype=jnp.float32) * 0.01, 'W2': jax.random.normal(ks[4], (E, F, D), dtype=jnp.float32) * scale_ff, 'b2': jax.random.normal(ks[5], (E, D), dtype=jnp.float32) * 0.01}
    _L2_ffn_all = _L2_ffn_setup()
    _L2_ffn_in = {k: v for k, v in _L2_ffn_all.items() if k in ('centroids', 'ln_g', 'ln_b', 'W1', 'b1', 'W2', 'b2')}
    del _L2_ffn_all

    def _L3_xattn_setup():
        import jax, jax.numpy as jnp
        import numpy as np
        D_MODEL = 128
        NUM_HEADS = 16
        D_K = D_MODEL // NUM_HEADS
        key = jax.random.key(seed)
        ks = jax.random.split(key, 12)
        B, S = (4, 256)
        scale = 1.0 / np.sqrt(D_MODEL)
        inp = {'query': jax.random.normal(ks[0], (B, S, D_MODEL), jnp.float32), 'key': jax.random.normal(ks[1], (B, S, D_MODEL), jnp.float32), 'value': jax.random.normal(ks[2], (B, S, D_MODEL), jnp.float32), 'Wq': jax.random.normal(ks[3], (NUM_HEADS, D_MODEL, D_K), jnp.float32) * scale, 'bq': jax.random.normal(ks[4], (NUM_HEADS, D_K), jnp.float32) * 0.01, 'Wk': jax.random.normal(ks[5], (NUM_HEADS, D_MODEL, D_K), jnp.float32) * scale, 'bk': jax.random.normal(ks[6], (NUM_HEADS, D_K), jnp.float32) * 0.01, 'Wv': jax.random.normal(ks[7], (NUM_HEADS, D_MODEL, D_K), jnp.float32) * scale, 'bv': jax.random.normal(ks[8], (NUM_HEADS, D_K), jnp.float32) * 0.01, 'Wo': jax.random.normal(ks[9], (NUM_HEADS * D_K, D_MODEL), jnp.float32) * scale, 'bo': jax.random.normal(ks[10], (D_MODEL,), jnp.float32) * 0.01}
        return inp
    _L3_xattn_all = _L3_xattn_setup()
    _L3_xattn_in = {k: v for k, v in _L3_xattn_all.items() if k in ('Wq', 'bq', 'Wk', 'bk', 'Wv', 'bv', 'Wo', 'bo')}
    del _L3_xattn_all

    def _L3_ffn_setup():
        import jax, jax.numpy as jnp
        import numpy as np
        B, S, D, FF, E, L = (8, 256, 128, 512, 16, 4)

        def _unipool_layer(xt, router, W1, W2):
            logits = xt @ router
            probs = jax.nn.softmax(logits, axis=-1)
            w = jnp.max(probs, axis=-1)
            idx = jnp.argmax(probs, axis=-1)

            def body(acc, params):
                w1, w2, i = params
                h = jax.nn.silu(xt @ w1) @ w2
                sel = jnp.where(idx == i, w, 0.0)
                return (acc + sel[:, None] * h, None)
            out, _ = jax.lax.scan(body, jnp.zeros_like(xt), (W1, W2, jnp.arange(W1.shape[0])))
            return out
        key = jax.random.key(seed)
        k0, k1, k2, k3 = jax.random.split(key, 4)
        x = jax.random.normal(k0, (B, S, D), dtype=jnp.float32)
        routers = jax.random.normal(k1, (L, D, E), dtype=jnp.float32) * 0.02
        W1 = jax.random.normal(k2, (E, D, FF), dtype=jnp.float32) * 0.02
        W2 = jax.random.normal(k3, (E, FF, D), dtype=jnp.float32) * 0.02
        return {'x': x, 'routers': routers, 'W1': W1, 'W2': W2}
    _L3_ffn_all = _L3_ffn_setup()
    _L3_ffn_in = {k: v for k, v in _L3_ffn_all.items() if k in ('routers', 'W1', 'W2')}
    del _L3_ffn_all
    return {'x': x, 'ctx_1024': ctx_1024, 'mask_Bx1xSxS2_bk0': mask_Bx1xSxS2_bk0, 'L0_xattn_Wq': _L0_xattn_in['Wq'], 'L0_xattn_Wk': _L0_xattn_in['Wk'], 'L0_xattn_Wv': _L0_xattn_in['Wv'], 'L0_xattn_Wo': _L0_xattn_in['Wo'], 'L0_ffn_Ws': _L0_ffn_in['Ws'], 'L0_ffn_bs': _L0_ffn_in['bs'], 'L0_ffn_W1': _L0_ffn_in['W1'], 'L0_ffn_b1': _L0_ffn_in['b1'], 'L0_ffn_W2': _L0_ffn_in['W2'], 'L0_ffn_b2': _L0_ffn_in['b2'], 'L1_xattn_W_q': _L1_xattn_in['W_q'], 'L1_xattn_W_k': _L1_xattn_in['W_k'], 'L1_xattn_W_v': _L1_xattn_in['W_v'], 'L1_xattn_W_proj': _L1_xattn_in['W_proj'], 'L1_xattn_b_proj': _L1_xattn_in['b_proj'], 'L1_ffn_w_gate': _L1_ffn_in['w_gate'], 'L1_ffn_w_up': _L1_ffn_in['w_up'], 'L1_ffn_w_down': _L1_ffn_in['w_down'], 'L2_xattn_Wq': _L2_xattn_in['Wq'], 'L2_xattn_bq': _L2_xattn_in['bq'], 'L2_xattn_Wkv': _L2_xattn_in['Wkv'], 'L2_xattn_bkv': _L2_xattn_in['bkv'], 'L2_xattn_Wo': _L2_xattn_in['Wo'], 'L2_xattn_bo': _L2_xattn_in['bo'], 'L2_ffn_centroids': _L2_ffn_in['centroids'], 'L2_ffn_ln_g': _L2_ffn_in['ln_g'], 'L2_ffn_ln_b': _L2_ffn_in['ln_b'], 'L2_ffn_W1': _L2_ffn_in['W1'], 'L2_ffn_b1': _L2_ffn_in['b1'], 'L2_ffn_W2': _L2_ffn_in['W2'], 'L2_ffn_b2': _L2_ffn_in['b2'], 'L3_xattn_Wq': _L3_xattn_in['Wq'], 'L3_xattn_bq': _L3_xattn_in['bq'], 'L3_xattn_Wk': _L3_xattn_in['Wk'], 'L3_xattn_bk': _L3_xattn_in['bk'], 'L3_xattn_Wv': _L3_xattn_in['Wv'], 'L3_xattn_bv': _L3_xattn_in['bv'], 'L3_xattn_Wo': _L3_xattn_in['Wo'], 'L3_xattn_bo': _L3_xattn_in['bo'], 'L3_ffn_routers': _L3_ffn_in['routers'], 'L3_ffn_W1': _L3_ffn_in['W1'], 'L3_ffn_W2': _L3_ffn_in['W2']}

def reference(x, ctx_1024, mask_Bx1xSxS2_bk0, L0_xattn_Wq, L0_xattn_Wk, L0_xattn_Wv, L0_xattn_Wo, L0_ffn_Ws, L0_ffn_bs, L0_ffn_W1, L0_ffn_b1, L0_ffn_W2, L0_ffn_b2, L1_xattn_W_q, L1_xattn_W_k, L1_xattn_W_v, L1_xattn_W_proj, L1_xattn_b_proj, L1_ffn_w_gate, L1_ffn_w_up, L1_ffn_w_down, L2_xattn_Wq, L2_xattn_bq, L2_xattn_Wkv, L2_xattn_bkv, L2_xattn_Wo, L2_xattn_bo, L2_ffn_centroids, L2_ffn_ln_g, L2_ffn_ln_b, L2_ffn_W1, L2_ffn_b1, L2_ffn_W2, L2_ffn_b2, L3_xattn_Wq, L3_xattn_bq, L3_xattn_Wk, L3_xattn_bk, L3_xattn_Wv, L3_xattn_bv, L3_xattn_Wo, L3_xattn_bo, L3_ffn_routers, L3_ffn_W1, L3_ffn_W2):
    import jax
    import jax.numpy as jnp

    def _L0_xattn_ref(queries, keys, values, Wq, Wk, Wv, Wo):
        import jax, jax.numpy as jnp
        import numpy as np
        NUM_HEADS = 16
        D_MODEL = 128
        NEG_INF = -1e+30

        def _split_heads(x, h):
            B, S, D = x.shape
            return x.reshape(B, S, h, D // h).transpose(0, 2, 1, 3)
        h = NUM_HEADS
        q = _split_heads(queries @ Wq, h)
        k = _split_heads(keys @ Wk, h)
        v = _split_heads(values @ Wv, h)
        dh = q.shape[-1]
        scores = jnp.einsum('bhqd,bhkd->bhqk', q, k) / jnp.sqrt(jnp.float32(dh))
        scores = jnp.where(scores == 0, NEG_INF, scores)
        attn = jax.nn.softmax(scores, axis=-1)
        out = jnp.einsum('bhqk,bhkd->bhqd', attn, v)
        B, _, S, _ = out.shape
        out = out.transpose(0, 2, 1, 3).reshape(B, S, h * dh)
        return out @ Wo

    def _L0_ffn_ref(x, Ws, bs, W1, b1, W2, b2):
        import jax, jax.numpy as jnp
        import numpy as np
        CAPACITY_FACTOR = 1.0
        B, S, D = x.shape
        E = Ws.shape[1]
        N = B * S
        k = int(CAPACITY_FACTOR * N / E)
        xf = x.reshape(N, D)
        route_prob = jax.nn.softmax(xf @ Ws + bs, axis=-1).T
        route_vals, routes = jax.lax.top_k(route_prob, k)
        xin = xf[routes]
        h = jax.nn.gelu(jnp.einsum('ekd,edf->ekf', xin, W1) + b1[:, None, :])
        out = jnp.einsum('ekf,efd->ekd', h, W2) + b2[:, None, :]
        out = out * route_vals[..., None]
        final = jnp.zeros((N, D), dtype=x.dtype).at[routes.reshape(-1)].add(out.reshape(-1, D))
        return final.reshape(B, S, D)

    def _L1_xattn_ref(queries, keys, values, mask, W_q, W_k, W_v, W_proj, b_proj):
        import jax, jax.numpy as jnp
        import numpy as np
        D_MODEL = 128
        N_HEADS = 16
        D_HEAD = D_MODEL // N_HEADS
        B = 4
        S = 256
        NEG_INF = -10000000000.0
        b, sq, _ = queries.shape
        Q = (queries @ W_q.T).reshape(b, sq, N_HEADS, D_HEAD).transpose(0, 2, 1, 3)
        K = (keys @ W_k.T).reshape(b, -1, N_HEADS, D_HEAD).transpose(0, 2, 1, 3)
        V = (values @ W_v.T).reshape(b, -1, N_HEADS, D_HEAD).transpose(0, 2, 1, 3)
        scale = jnp.sqrt(jnp.float32(D_HEAD))
        scores = jnp.einsum('bhqd,bhkd->bhqk', Q, K) / scale
        scores = jnp.where(mask, scores, NEG_INF)
        attention = jax.nn.softmax(scores, axis=-1)
        heads_out = jnp.einsum('bhqk,bhkd->bhqd', attention, V)
        heads_out = heads_out.transpose(0, 2, 1, 3).reshape(b, sq, D_MODEL)
        out = heads_out @ W_proj.T + b_proj
        return out

    def _L1_ffn_ref(x, w_gate, w_up, w_down):
        import jax, jax.numpy as jnp
        import numpy as np
        BLOCK = 32
        W_BITS = 4
        ACT_BITS = 16

        def act_qdq(x):
            qmax = 2.0 ** (ACT_BITS - 1) - 1.0
            scale = jnp.maximum(jnp.max(jnp.abs(x)) / qmax, 1e-12)
            return jnp.clip(jnp.round(x / scale), -qmax - 1.0, qmax) * scale

        def fixed_qdq_u16(x):
            scale = 1.0 / 65536.0
            return jnp.clip(jnp.round(x / scale), 0.0, 65535.0) * scale

        def lpbq_dequant(w):
            O, I = w.shape
            qmax = 2.0 ** (W_BITS - 1) - 1.0
            wb = w.reshape(O, I // BLOCK, BLOCK)
            s = jnp.maximum(jnp.max(jnp.abs(wb), axis=-1, keepdims=True) / qmax, 1e-12)
            wq = jnp.clip(jnp.round(wb / s), -qmax - 1.0, qmax) * s
            return wq.reshape(O, I)
        x = act_qdq(x)
        up = act_qdq(x @ lpbq_dequant(w_up).T)
        gate = act_qdq(x @ lpbq_dequant(w_gate).T)
        sig = fixed_qdq_u16(jax.nn.sigmoid(gate))
        gate = act_qdq(gate * sig)
        o = act_qdq(gate * up)
        return o @ lpbq_dequant(w_down).T

    def _L2_xattn_ref(query, key_value, Wq, bq, Wkv, bkv, Wo, bo):
        import jax, jax.numpy as jnp
        import numpy as np
        B, SQ, SK, D, H = (4, 256, 256, 128, 16)
        HD = D // H
        b, sq, _ = query.shape
        sk = key_value.shape[1]
        Q = (query @ Wq + bq).reshape(b, sq, H, HD).transpose(0, 2, 1, 3)
        KV = (key_value @ Wkv + bkv).reshape(b, sk, 2, H, HD)
        K = KV[:, :, 0].transpose(0, 2, 1, 3)
        V = KV[:, :, 1].transpose(0, 2, 1, 3)
        scale = 1.0 / np.sqrt(HD).astype(np.float32)
        scores = jnp.einsum('bhqd,bhkd->bhqk', Q, K) * scale
        attn = jax.nn.softmax(scores, axis=-1)
        out = jnp.einsum('bhqk,bhkd->bhqd', attn, V)
        out = out.transpose(0, 2, 1, 3).reshape(b, sq, D)
        return out @ Wo + bo

    def _L2_ffn_ref(input_features, centroids, ln_g, ln_b, W1, b1, W2, b2):
        import jax, jax.numpy as jnp
        import numpy as np
        E = 8
        D = 128
        F = 512
        S, B = (256, 2)
        LN_EPS = 1e-05

        def _moe_forward(input_features, centroids, ln_g, ln_b, W1, b1, W2, b2):
            s, b, d = input_features.shape
            x = jnp.swapaxes(input_features, 0, 1).reshape(-1, d)
            logits = x.astype(jnp.float32) @ centroids.astype(jnp.float32).T
            assign = jnp.argmax(logits, axis=-1)
            onehot = jax.nn.one_hot(assign, E, dtype=x.dtype)
            disp = jnp.einsum('te,td->etd', onehot, x)
            mu = disp.mean(-1, keepdims=True)
            var = disp.var(-1, keepdims=True)
            xn = (disp - mu) * jax.lax.rsqrt(var + LN_EPS)
            xn = xn * ln_g[:, None, :] + ln_b[:, None, :]
            h = jax.nn.relu(jnp.einsum('etd,edf->etf', xn, W1) + b1[:, None, :])
            y = jnp.einsum('etf,efd->etd', h, W2) + b2[:, None, :]
            y = disp + y
            out = jnp.einsum('te,etd->td', onehot, y)
            return jnp.swapaxes(out.reshape(b, s, d), 0, 1)
        return _moe_forward(input_features, centroids, ln_g, ln_b, W1, b1, W2, b2)

    def _L3_xattn_ref(query, key, value, Wq, bq, Wk, bk, Wv, bv, Wo, bo):
        import jax, jax.numpy as jnp
        import numpy as np
        D_MODEL = 128
        NUM_HEADS = 16
        D_K = D_MODEL // NUM_HEADS
        q = jnp.einsum('bsd,hdk->bhsk', query, Wq) + bq[None, :, None, :]
        k = jnp.einsum('bsd,hdk->bhsk', key, Wk) + bk[None, :, None, :]
        v = jnp.einsum('bsd,hdk->bhsk', value, Wv) + bv[None, :, None, :]
        scores = jnp.einsum('bhqk,bhsk->bhqs', q, k) / jnp.sqrt(jnp.asarray(D_K, q.dtype))
        attn = jax.nn.softmax(scores, axis=-1)
        heads = jnp.einsum('bhqs,bhsk->bhqk', attn, v)
        B, H, S, K = heads.shape
        concat = jnp.transpose(heads, (0, 2, 1, 3)).reshape(B, S, H * K)
        return concat @ Wo + bo

    def _L3_ffn_ref(x, routers, W1, W2):
        import jax, jax.numpy as jnp
        import numpy as np
        B, S, D, FF, E, L = (8, 256, 128, 512, 16, 4)

        def _unipool_layer(xt, router, W1, W2):
            logits = xt @ router
            probs = jax.nn.softmax(logits, axis=-1)
            w = jnp.max(probs, axis=-1)
            idx = jnp.argmax(probs, axis=-1)

            def body(acc, params):
                w1, w2, i = params
                h = jax.nn.silu(xt @ w1) @ w2
                sel = jnp.where(idx == i, w, 0.0)
                return (acc + sel[:, None] * h, None)
            out, _ = jax.lax.scan(body, jnp.zeros_like(xt), (W1, W2, jnp.arange(W1.shape[0])))
            return out
        b, s, d = x.shape
        xt = x.reshape(-1, d)

        def step(carry, router):
            return (_unipool_layer(carry, router, W1, W2), None)
        xt, _ = jax.lax.scan(step, xt, routers)
        return xt.reshape(b, s, d)
    x = x + _L0_xattn_ref(_layernorm(x, axis=-1), ctx_1024, ctx_1024, L0_xattn_Wq, L0_xattn_Wk, L0_xattn_Wv, L0_xattn_Wo)
    x = x + _L0_ffn_ref(_layernorm(x, axis=-1), L0_ffn_Ws, L0_ffn_bs, L0_ffn_W1, L0_ffn_b1, L0_ffn_W2, L0_ffn_b2)
    x = x + _L1_xattn_ref(_layernorm(x, axis=-1), ctx_1024, ctx_1024, mask_Bx1xSxS2_bk0, L1_xattn_W_q, L1_xattn_W_k, L1_xattn_W_v, L1_xattn_W_proj, L1_xattn_b_proj)
    x = x + _L1_ffn_ref(_layernorm(x, axis=-1), L1_ffn_w_gate, L1_ffn_w_up, L1_ffn_w_down)
    x = x + _L2_xattn_ref(_layernorm(x, axis=-1), ctx_1024, L2_xattn_Wq, L2_xattn_bq, L2_xattn_Wkv, L2_xattn_bkv, L2_xattn_Wo, L2_xattn_bo)
    x = x + _L2_ffn_ref(_layernorm(x, axis=-1), L2_ffn_centroids, L2_ffn_ln_g, L2_ffn_ln_b, L2_ffn_W1, L2_ffn_b1, L2_ffn_W2, L2_ffn_b2)
    x = x + _L3_xattn_ref(_layernorm(x, axis=-1), ctx_1024, ctx_1024, L3_xattn_Wq, L3_xattn_bq, L3_xattn_Wk, L3_xattn_bk, L3_xattn_Wv, L3_xattn_bv, L3_xattn_Wo, L3_xattn_bo)
    x = x + _L3_ffn_ref(_layernorm(x, axis=-1), L3_ffn_routers, L3_ffn_W1, L3_ffn_W2)
    return x

_drawn_inputs = setup_inputs


def setup_inputs(seed=0):
    import zlib

    import numpy as np

    out = dict(_drawn_inputs(seed))
    spreads = {'L0_ffn_bs': (0.0, 0.1),
     'L0_ffn_b1': (0.0, 0.1),
     'L0_ffn_b2': (0.0, 0.1),
     'L1_xattn_b_proj': (0.0, 0.1),
     'L2_xattn_bq': (0.0, 0.1),
     'L2_xattn_bkv': (0.0, 0.1),
     'L2_xattn_bo': (0.0, 0.1),
     'L2_ffn_ln_g': (1.0, 0.2),
     'L2_ffn_ln_b': (0.0, 0.292)}
    factors = {'L2_ffn_b1': 21.338,
     'L2_ffn_b2': 8.0,
     'L3_xattn_bq': 63.245,
     'L3_xattn_bk': 200.0,
     'L3_xattn_bv': 8.0,
     'L3_xattn_bo': 8.0}
    for name, (base, spread) in spreads.items():
        noise = np.random.default_rng([zlib.crc32(name.encode()), seed]).standard_normal(out[name].shape)
        drawn = base * np.exp(spread * noise) if base else spread * noise
        out[name] = jnp.asarray(drawn.astype(out[name].dtype))
    for name, factor in factors.items():
        out[name] = (out[name] * factor).astype(out[name].dtype)
    return out
```

```python
import concourse.bass as bass
from concourse import mybir
from contextlib import ExitStack

F32 = mybir.dt.float32
BF16 = mybir.dt.bfloat16
I32 = mybir.dt.int32
U32 = mybir.dt.uint32
U8 = mybir.dt.uint8
ALU = mybir.AluOpType
ACT = mybir.ActivationFunctionType
AX = mybir.AxisListType

P = 128
B = 8
D = 128
H, DH = 16, 8
ROWS = 16
HC = 8
F = 512
FC = F // P
QF = 384
QC = QF // P
E8, E16 = 8, 16
NB8 = B + E8 - 1
NB16 = B + E16 - 1
CAP = 128
NT = 4
FILL = -(2.0 ** 100)
SCALE = float(DH) ** -0.5
EPS = 1e-5
MAGIC = 1.5 * 2.0 ** 23
QMAX = 32767.0
WMAX = 7.0
TINY = 1e-12


class Link:

    def __init__(self, sem):
        self.sem, self.n, self.turn = sem, 0, 0

    def __call__(self, eng, ins):
        ins.then_inc(self.sem, 1)
        self.n += 1
        eng.wait_ge(self.sem, self.turn + self.n)

    def enter(self, i, start, per):
        self.at, self.per, self.turn = self.n, per, (i - start) * per

    def leave(self, turns):
        assert self.n - self.at == self.per, (self.n - self.at, self.per)
        self.n, self.turn = self.at + self.per * turns, 0


class Mix:

    def __init__(self, layer, kind, E, nb, before, par, xt, logits, exps, route):
        self.layer, self.kind, self.E, self.nb = layer, kind, E, nb
        self.before, self.par = before, par
        self.xt, self.logits, self.exps, self.route = xt, logits, exps, route

    def stored(self, j, p):
        return 16 * self.par[p] + 8 * (j - p)

    def all_stored(self, p):
        return 16 * (self.par[p] + (self.nb + 1 - p) // 2)


M0 = Mix(0, "gelu", E8, B, 0, (0, 0), 1, 0, 0, None)
M1 = Mix(2, "relu", E8, NB8, B, (0, 0), 5, 1, 1, 0)
MC = [Mix(3, "silu", E16, NB16, B + NB8 + NB16 * i, ((NB8 + 1) // 2 + (NB16 + 1) // 2 * i, NB8 // 2 + NB16 // 2 * i),
          7 + i, 2 + i, 1 + i, 1 + i) for i in range(NT)]


def build(nc, a, out):
    ctx = ExitStack()
    with ctx:
        def sb(name, shape, dt=F32):
            return ctx.enter_context(nc.sbuf_tensor(name, shape, dt))

        sems = {}

        def S(name):
            if name not in sems:
                sems[name] = ctx.enter_context(nc.semaphore(name))
            return sems[name]

        def due(n):
            return not (isinstance(n, int) and n <= 0)

        x = sb("x", [P, B, D])
        xn = sb("xn", [P, B, D])
        xnT = sb("xnT", [P, B * P])
        ctxT = sb("ctxT", [P, B * P])
        KT = sb("KT", [P, 2, B, P])
        Va = sb("Va", [P, B, H, DH + 1])
        Qs = sb("Qs", [P, 2, P])
        Ks = sb("Ks", [P, 2, P])
        Qa = sb("Qa", [P, 2, P])
        Mp = sb("Mp", [P, H, ROWS])
        rs = sb("rs", [P, H])
        sel = sb("sel", [P, 4, DH + 1])
        o_sb = sb("o_sb", [P, D])
        oT = sb("oT", [P, P])
        scr = sb("scr", [P, 3 * QC * B * P])
        PT = scr[:, 0:2 * HC * P].rearrange("p (c n) -> p c n", c=2)
        QT = scr[:, 2048:4096].rearrange("p (c b q) -> p c b q", c=2, b=B)
        Km = scr[:, 4096:6144].rearrange("p (c j k) -> p c j k", c=2, j=HC)
        Qm = scr[:, 6144:8192].rearrange("p (c j q) -> p c j q", c=2, j=HC)
        ind = scr[:, 8192:9216].bitcast(BF16).rearrange("p (c n) -> p c n", c=2)
        wraw = scr[:, 7168:8448].rearrange("p (n d) -> p n d", n=10)
        work = scr[0:E8, 4096:5120]
        wqr = scr[:, 2048:3200].rearrange("p (n k) -> p n k", n=3)
        brow = scr[0:1, 4096:6144].rearrange("p (n h r) -> p n h r", n=8, h=H)
        craw = scr[:, 0:B * D].rearrange("p (b d) -> p b d", b=B)
        fill = sb("fill", [P, B, P], BF16)
        mask8 = sb("mask8", [P, B, P], U8)
        wq = sb("wq", [P, 4, H, ROWS])
        wk = sb("wk", [P, 4, H, ROWS])
        wv = sb("wv", [P, 4, D])
        wo = sb("wo", [P, 4, D])
        bcol = sb("bcol", [P, 8, 2])
        bv = sb("bv", [P, 2, D])
        bo = sb("bo", [P, 3, D])
        ident = sb("ident", [P, P])
        identb = sb("identb", [P, P], BF16)
        tri = sb("tri", [P, P], BF16)
        ones = sb("ones", [P, P])
        onesb = sb("onesb", [P, P], BF16)
        hmask = sb("hmask", [P, HC])
        half = sb("half", [P, B])
        stats = sb("stats", [P, B, 6])
        mv = sb("mv", [P, B, 2])
        rstd = sb("rstd", [P, B])

        big = sb("big", [P, 4 * E8 * F])
        W1 = {0: big[:, 0:E8 * F], 2: big[:, 2 * E8 * F:3 * E8 * F], 3: big[:, 0:E16 * F]}
        W2 = {0: big[:, E8 * F:2 * E8 * F], 2: big[:, 3 * E8 * F:4 * E8 * F], 3: big[:, E16 * F:2 * E16 * F]}
        b1r = sb("b1r", [P, E8, F])
        b2r = sb("b2r", [P, 2, E8, D])
        lnT = sb("lnT", [P, 2, E8])
        b8 = sb("b8", [E8, F])
        e8w = sb("e8w", [E8, 3, D])
        rw = sb("rw", [P, 2, E8])
        rw16 = sb("rw16", [P, NT, E16])
        bs8 = sb("bs8", [P, E8])
        lg = sb("lg", [P, B * E16])
        lt = sb("lt", [P, B * E16])
        ohb = sb("ohb", [P, B * E16], BF16)
        r1 = sb("r1", [P, B])
        wtop = sb("wtop", [P, B])
        erev = sb("erev", [P, E16])
        c1 = sb("c1", [P, E16])
        c2 = sb("c2", [P, E16])
        ci = sb("ci", [P, E16], I32)
        slotf = sb("slotf", [P, B])
        slot = sb("slot", [P, B], I32)
        jrow = sb("jrow", [1, 24])
        iot = sb("iot", [P, 24], I32)
        jcmp = sb("jcmp", [1, 24, E16])
        bef = sb("bef", [1, 24])
        be = sb("be", [1, 24], I32)
        xs = sb("xs", [P, 2, D])
        xsT = sb("xsT", [P, 2, P])
        hb = sb("hb", [P, F])
        hs = sb("hs", [P, F])
        oU = hb
        Vs = hs[:, 0:H * (DH + 1)]
        hT = sb("hT", [P, F])
        yb = sb("yb", [P, D])
        ys = sb("ys", [P, 2, D])
        top = sb("top", [E8, 2, CAP])
        topi = sb("topi", [E8, CAP], U32)
        idx = sb("idx", [P, E8], I32)
        rv = sb("rv", [P, E8])
        xn2 = scr[:, 2048:3072].rearrange("p (b d) -> p b d", b=B)
        yg = scr[:, 3072:4096].rearrange("p (b d) -> p b d", b=B)
        xs_d = nc.dram_tensor("xs_d", (NB16 * P, D), F32, kind="Internal").ap()
        ys_d = nc.dram_tensor("ys_d", (NB16 * P, D), F32, kind="Internal").ap()
        xn_d = nc.dram_tensor("xn_d", (B * P, D), F32, kind="Internal").ap()
        acc_d = nc.dram_tensor("acc_d", (B * P, D), F32, kind="Internal").ap()

        wqT = sb("wqT", [P, 3, QF])
        wsc = sb("wsc", [P, 36])
        wrc = sb("wrc", [P, 36])
        am = sb("am", [P, 7])
        qrow = sb("qrow", [1, 1])
        qs = sb("qs", [P, 4, 2])
        qo = sb("qo", [P, 3, 2])
        QG, QU, QV = (scr[:, QC * B * P * n:QC * B * P * (n + 1)] for n in range(3))

        psum = ctx.enter_context(nc.psum_tensor("psum", [P, 8, 512], F32))
        bank = [psum[:, n, :] for n in range(8)]

        Qmf = [Qm[:, c, :, :].rearrange("p j q -> p (j q)") for c in range(2)]
        Kmf = [Km[:, c, :, :].rearrange("p j q -> p (j q)") for c in range(2)]
        Mpf = Mp[:, :, :].rearrange("p h r -> p (h r)")
        avs = bank[6][:, 0:H * (DH + 1)].rearrange("p (h n) -> p h n", h=H)
        VB = {2: 0, 3: 1}
        OB = {1: 0, 2: 1, 3: 2}
        PAD = [("wq", 0, 0), ("wk", 0, 1), ("wq", 2, 2), ("wk", 2, 3), ("wq", 3, 4), ("wk", 3, 5)]

        def pool_rstd(pool, link, n):
            pool.wait_ge(S("var_ready"), n + 1)
            link(pool, pool.tensor_scalar(rstd[:, :], mv[:, :, 1], EPS, None, ALU.add))
            pool.tensor_tensor(rstd[:, :], rstd[:, :], half[:, :], ALU.pow).then_inc(S("rstd_ready"), 1)

        def pool_attention(pool, L):
            n0 = B * L

            def keys(i):
                if due(n0 + i):
                    pool.wait_ge(S("weights_ps1"), n0 + i)
                pool.tensor_copy(Ks[:, :, :], KT[:, :, bass.ds(i, 1), :].rearrange("p c a k -> p c (a k)")
                                 ).then_inc(S("ks_ready"), 1)

            def values(i):
                if due(n0 + i):
                    pool.wait_ge(S("av1"), n0 + i)
                pool.tensor_copy(Vs, Va[:, bass.ds(i, 1), :, :].rearrange("p a h n -> p (a h n)")
                                 ).then_inc(S("vs_ready"), 1)

            def scores_operands(i):
                if due(n0 + i):
                    pool.wait_ge(S("scores1"), n0 + i)
                pool.tensor_copy(Qs[:, :, :], QT[:, :, bass.ds(i, 1), :].rearrange("p c a k -> p c (a k)"))
                pool.tensor_tensor(Km[:, :, :, :], KT[:, :, bass.ds(i, 1), :].to_broadcast([P, 2, HC, P]),
                                   hmask[:, :].unsqueeze(1).unsqueeze(3).to_broadcast([P, 2, HC, P]), ALU.mult
                                   ).then_inc(S("qk_ready"), 1)

            pool.wait_ge(S("k_copied"), 4 * L + 4)
            pool.wait_ge(S("q_copied"), 4 * L + 4)
            scores_operands(0)
            keys(0)
            pool.wait_ge(S("v_copied"), L + 1)
            values(0)
            scores_operands(1)
            with pool.Fori(1, B - 1) as i:
                keys(i)
                values(i)
                scores_operands(i + 1)
            keys(B - 1)
            values(B - 1)

        def act_xnT(act, m):
            for n in range(2):
                act.wait_ge(S("xnT_ps"), 2 * m + n + 1)
                act.activation(xnT[:, 512 * n:512 * n + 512], bank[n], ACT.Copy).then_inc(S("xnT_copied"), 1)

        def act_attention(act, L):
            n0 = B * L

            def copies(dst, src_sem, done, row):
                for n in range(4):
                    h, c = n // 2, n % 2
                    act.wait_ge(S(src_sem), 4 * L + n + 1)
                    act.activation(dst[:, c, 4 * h:4 * h + 4, :].rearrange("p b k -> p (b k)"), bank[4 + n],
                                   ACT.Identity, bias=bcol[:, row, c:c + 1]).then_inc(S(done), 1)

            def exp(i, c):
                act.wait_ge(S(f"weights_ps{c}"), n0 + i + 1)
                if due(n0 + i):
                    act.wait_ge(S(f"av{c}"), n0 + i)
                act.activation(PT[:, c, :], psum[:, 4:6, :].rearrange("p a n -> p (a n)"), ACT.Exp, scale=SCALE
                               ).then_inc(S(f"exp{c}"), 1)

            def copy_oT(i):
                act.wait_ge(S("oT_ps"), n0 + i + 1)
                if due(n0 + i):
                    act.wait_ge(S("proj_ps"), n0 + i)
                act.activation(oT[:, :], bank[6][:, 256:384], ACT.Copy).then_inc(S("oT_copied"), 1)

            def copy_oU(i):
                act.wait_ge(S("av1"), n0 + i + 1)
                if due(n0 + i):
                    act.wait_ge(S("avs_ps"), n0 + i)
                act.activation(oU[:, :], bank[7], ACT.Copy).then_inc(S("oU_copied"), 1)

            copies(KT, "k_ps", "k_copied", 4 + L)
            act_xnT(act, XT[L])
            copies(QT, "q_ps", "q_copied", L)
            exp(0, 0)
            exp(0, 1)
            with act.Fori(1, B) as i:
                copy_oU(i - 1)
                exp(i, 0)
                exp(i, 1)
                copy_oT(i - 1)
            copy_oU(B - 1)
            copy_oT(B - 1)

        def dve_layernorm(dve, link, n, src, dst):
            for b in range(B):
                last = dve.bn_stats(stats[:, b, :], src[:, b, :])
            link(dve, last)
            for b in range(B):
                last = dve.bn_aggr(mv[:, b, :], stats[:, b, :])
            last.then_inc(S("var_ready"), 1)
            dve.wait_ge(S("rstd_ready"), n + 1)
            for b in range(B):
                dve.tensor_scalar(dst[:, b, :], src[:, b, :], mv[:, b, 0:1], rstd[:, b:b + 1],
                                  ALU.subtract, ALU.mult).then_inc(S("xn_ready"), 1)

        def dve_attention(dve, link, L):
            n0 = B * L

            def values():
                dve.wait_ge(S("ld_bo"), 16 * 5)
                for n in range(2):
                    dve.wait_ge(S("v_ps"), 2 * L + n + 1)
                    src = bank[2 + n].rearrange("p (b h d) -> p b h d", b=4, h=H)
                    dst = Va[:, 4 * n:4 * n + 4, :, 0:DH]
                    if L in VB:
                        for b in range(4):
                            last = dve.tensor_tensor(dst[:, b], src[:, b],
                                                     bv[:, VB[L], :].rearrange("p (h d) -> p h d", h=H), ALU.add)
                    else:
                        last = dve.tensor_copy(dst, src)
                last.then_inc(S("v_copied"), 1)
                dve.wait_ge(S("q_copied"), 4 * L + 4)
                dve.memset(bank[7], 0.0).then_inc(S("bank7_clear"), 1)

            def masked_queries(i):
                dve.wait_ge(S("max_ps"), n0 + i + 1)
                link(dve, dve.tensor_tensor(Qa[:, :, :], bank[4][:, 0:256].rearrange("p (c q) -> p c q", c=2),
                                            QT[:, :, bass.ds(i, 1), :].rearrange("p c a q -> p c (a q)"), ALU.add))
                if due(n0 + i):
                    dve.wait_ge(S("weights_ps1"), n0 + i)
                for c in range(2):
                    dve.tensor_tensor(Qm[:, c, :, :], Qa[:, c, :].unsqueeze(1).to_broadcast([P, HC, P]),
                                      hmask[:, :].unsqueeze(2).to_broadcast([P, HC, P]), ALU.mult
                                      ).then_inc(S("qm_ready"), 1)

            def normalise(i):
                dve.wait_ge(S("avs_ps"), n0 + i + 1)
                link(dve, dve.reciprocal(rs[:, :].unsqueeze(2), avs[:, :, DH:DH + 1]))
                if due(n0 + i):
                    dve.wait_ge(S("oT_ps"), n0 + i)
                dve.tensor_tensor(o_sb[:, :].rearrange("p (h d) -> p h d", h=H), avs[:, :, 0:DH],
                                  rs[:, :].unsqueeze(2).to_broadcast([P, H, DH]), ALU.mult
                                  ).then_inc(S("o_ready"), 1)

            def maxima(i, c):
                raw = psum[:, 2 * c:2 * c + 2, :]
                dve.wait_ge(S(f"scores{c}"), n0 + i + 1)
                if L == 0:
                    dve.tensor_scalar(ind[:, c, :], raw.rearrange("p a n -> p (a n)"), 0.0, FILL,
                                      ALU.is_equal, ALU.mult).then_inc(S(f"zeros{c}"), 1)
                    dve.wait_ge(S(f"masked{c}"), i + 1)
                if due(n0 + i):
                    dve.wait_ge(S("max_ps"), n0 + i)
                dve.tensor_reduce(Mp[:, HC * c:HC * c + HC, DH:DH + 1],
                                  raw.rearrange("p a (j k) -> p (a j) k", j=4), AX.X, ALU.max, negate=True
                                  ).then_inc(S(f"max{c}"), 1)

            def residual(i):
                dve.wait_ge(S("proj_ps"), n0 + i + 1)
                xi = x[:, bass.ds(i, 1), :].rearrange("p a d -> p (a d)")
                ins = dve.tensor_tensor(xi, xi, bank[6][:, 384:512], ALU.add)
                if L in OB:
                    link(dve, ins)
                    ins = dve.tensor_tensor(xi, xi, bo[:, OB[L], :], ALU.add)
                ins.then_inc(S("x_res"), 1)

            values()
            maxima(0, 0)
            maxima(0, 1)

            def body(i, first=False, last=False):
                masked_queries(i)
                if not first:
                    normalise(i - 1)
                if not last:
                    maxima(i + 1, 0)
                    maxima(i + 1, 1)
                if not first:
                    residual(i - 1)

            body(0, first=True)
            with dve.Fori(1, B - 1) as i:
                link.enter(i, 1, 2 + (L in OB))
                body(i)
                link.leave(B - 2)
            body(B - 1, last=True)
            normalise(B - 1)
            residual(B - 1)
            dve.wait_ge(S("x_res"), n0 + B)

        def pe_xnT(pe, m, ready, n, each=1):
            for b in range(B):
                pe.wait_ge(S(ready), n + each * b + 1)
                ins = pe.transpose(bank[b // 4][:, P * (b % 4):P * (b % 4) + P], xn[:, b, :], ident[:, :])
                if b % 4 == 3:
                    ins.then_inc(S("xnT_ps"), 1)

        def pe_attention(pe, L):
            n0 = B * L
            if L == 1:
                pe.wait_ge(S("y_ready"), M0.nb)
            if L == 2:
                pe.wait_ge(S("x_quantised"), 2)
                pe.wait_ge(S("b1_folded"), E8)
            if L == 3:
                pe.wait_ge(S("y_ready"), M0.nb + M1.nb)

            def project(w, src, n):
                h, c = n // 2, n % 2
                return pe.matmul(bank[4 + n], w[:, L, HC * c:HC * c + HC, :].rearrange("p h r -> p (h r)"),
                                 src[:, 512 * h:512 * h + 512], start=True, stop=True)

            def scores(i, c):
                pe.wait_ge(S("qk_ready"), n0 + i + 1)
                if due(n0 + i):
                    pe.wait_ge(S(f"max{c}"), n0 + i)
                for r in range(2):
                    ins = pe.matmul(bank[2 * c + r], Qs[:, c, :], Kmf[c][:, 512 * r:512 * r + 512], start=True, stop=L > 1,
                                    skip_group_check=L < 2)
                if L == 1:
                    for r in range(2):
                        ins = pe.matmul(bank[2 * c + r].rearrange("p (j k) -> p j k", j=4), identb[:, :],
                                        fill[:, bass.ds(i, 1), :].to_broadcast([P, 4, P]),
                                        start=False, stop=True, skip_group_check=True)
                ins.then_inc(S(f"scores{c}"), 1)

            def mask_zeros(i, c):
                pe.wait_ge(S(f"zeros{c}"), i + 1)
                for r in range(2):
                    ins = pe.matmul(bank[2 * c + r], identb[:, :], ind[:, c, 512 * r:512 * r + 512],
                                    start=False, stop=True, skip_group_check=True)
                ins.then_inc(S(f"masked{c}"), 1)

            def maxima(i):
                pe.wait_ge(S("max0"), n0 + i + 1)
                pe.wait_ge(S("max1"), n0 + i + 1)
                if due(n0 + i):
                    pe.wait_ge(S("exp1"), n0 + i)
                for c in range(2):
                    ins = pe.transpose(bank[4][:, P * c:P * c + P], Mpf[:, P * c:P * c + P], ident[:, :])
                ins.then_inc(S("max_ps"), 1)

            def weights(i, c):
                pe.wait_ge(S("qm_ready"), 2 * (n0 + i) + c + 1)
                if c == 0:
                    pe.wait_ge(S("ks_ready"), n0 + i + 1)
                    if due(n0 + i):
                        pe.wait_ge(S("exp1"), n0 + i)
                else:
                    pe.wait_ge(S("exp0"), n0 + i + 1)
                for r in range(2):
                    ins = pe.matmul(bank[4 + r], Ks[:, c, :], Qmf[c][:, 512 * r:512 * r + 512], start=True, stop=L > 1,
                                    skip_group_check=L < 2)
                for r in range(2):
                    if L == 0:
                        for j in range(4):
                            k = P * (4 * r + j)
                            ins = pe.matmul(bank[4 + r][:, P * j:P * j + P], ind[:, c, k:k + P], identb[:, :],
                                            start=False, stop=True, skip_group_check=True)
                    if L == 1:
                        ins = pe.matmul(bank[4 + r].rearrange("p (j k) -> p j k", j=4),
                                        fill[:, bass.ds(i, 1), :].rearrange("p a k -> p (a k)"),
                                        identb[:, :].unsqueeze(1).to_broadcast([P, 4, P]),
                                        start=False, stop=True, skip_group_check=True)
                ins.then_inc(S(f"weights_ps{c}"), 1)

            def attend(i, c):
                pe.wait_ge(S(f"exp{c}"), n0 + i + 1)
                if c == 0:
                    pe.wait_ge(S("vs_ready"), n0 + i + 1)
                    if due(n0 + i):
                        pe.wait_ge(S("oU_copied"), n0 + i)
                for h in range(HC):
                    g, j = (HC * c + h) // 4, h % 4
                    v = (DH + 1) * (HC * c + h)
                    ins = pe.matmul(bank[7][32 * j:32 * j + DH + 1, P * g:P * g + P], Vs[:, v:v + DH + 1],
                                    PT[:, c, P * h:P * h + P], start=True, stop=True)
                ins.then_inc(S(f"av{c}"), 1)

            def turn_outputs(i):
                pe.wait_ge(S("oU_copied"), n0 + i + 1)
                if due(n0 + i):
                    pe.wait_ge(S("x_res"), n0 + i)
                for g in range(4):
                    w = 4 * (DH + 1)
                    ins = pe.matmul(bank[6][:, w * g:w * g + w], oU[:, P * g:P * g + P],
                                    sel[:, :, :].rearrange("p j n -> p (j n)"), start=True, stop=True)
                ins.then_inc(S("avs_ps"), 1)

            def out_transpose(i):
                pe.wait_ge(S("o_ready"), n0 + i + 1)
                pe.transpose(bank[6][:, 256:384], o_sb[:, :], ident[:, :]).then_inc(S("oT_ps"), 1)

            def out_project(i):
                pe.wait_ge(S("oT_copied"), n0 + i + 1)
                pe.matmul(bank[6][:, 384:512], oT[:, :], wo[:, L, :], start=True, stop=True
                          ).then_inc(S("proj_ps"), 1)

            for n in range(4):
                project(wk, ctxT, n).then_inc(S("k_ps"), 1)
            for b in range(B):
                ins = pe.matmul(bank[2 + b // 4][:, P * (b % 4):P * (b % 4) + P], ctxT[:, P * b:P * b + P],
                                wv[:, L, :], start=True, stop=True)
                if b % 4 == 3:
                    ins.then_inc(S("v_ps"), 1)
            pe_xnT(pe, XT[L], "xn_ready", XR[L])
            for n in range(4):
                pe.wait_ge(S("xnT_copied"), 2 * XT[L] + n // 2 + 1)
                pe.wait_ge(S("k_copied"), 4 * L + n + 1)
                project(wq, xnT, n).then_inc(S("q_ps"), 1)
            pe.wait_ge(S("bank7_clear"), L + 1)

            def body(i, first=False, last=False):
                maxima(i)
                if not first:
                    attend(i - 1, 1)
                weights(i, 0)
                if not first:
                    turn_outputs(i - 1)
                if not last:
                    scores(i + 1, 0)
                    scores(i + 1, 1)
                weights(i, 1)
                if not first:
                    out_transpose(i - 1)
                if L == 0 and not last:
                    mask_zeros(i + 1, 0)
                    mask_zeros(i + 1, 1)
                attend(i, 0)
                if not first:
                    out_project(i - 1)

            for c in range(2):
                scores(0, c)
            if L == 0:
                for c in range(2):
                    mask_zeros(0, c)
            body(0, first=True)
            with pe.Fori(1, B - 1) as i:
                body(i)
            body(B - 1, last=True)
            attend(B - 1, 1)
            turn_outputs(B - 1)
            out_transpose(B - 1)
            out_project(B - 1)

        def steps(eng, nb, first, last, step, link=None, per=0):
            pairs = (nb - 3) // 2
            for j in range(first, 2):
                step(j, j % 2, lambda d, j=j: 0 <= j + d < nb)
            with eng.Fori(0, pairs) as t:
                if link:
                    link.enter(t, 0, 2 * per)
                for p in range(2):
                    step(2 + 2 * t + p, p, lambda d: True)
                if link:
                    link.leave(pairs)
            for j in range(2 + 2 * pairs, last):
                step(j, j % 2, lambda d, j=j: 0 <= j + d < nb)

        def expert(eng, m, j):
            if m.kind == "gelu":
                return j
            return eng.value_load(be[0:1, bass.ds(j, 1)], min_val=0, max_val=m.E - 1)

        def pe_blocks(pe, m):
            n0 = m.before
            w1, w2 = W1[m.layer], W2[m.layer]

            def tokens(j, p):
                pe.wait_ge(S(f"gathered{p}" if m.kind == "gelu" else f"xs_ld{p}"), m.stored(j, p) + 16)
                if due(n0 + j):
                    pe.wait_ge(S("xsT_copied"), n0 + j)
                pe.transpose(bank[0][:, 0:P], xs[:, p, :], ident[:, :]).then_inc(S("xsT_ps"), 1)

            def hidden(j, p):
                e = expert(pe, m, j)
                pe.wait_ge(S("xsT_copied"), n0 + j + 1)
                pe.matmul(bank[1], xsT[:, p, :], w1[:, bass.ds(e * F, F)], start=True, stop=True
                          ).then_inc(S("h_ps"), 1)

            def transposes(j):
                pe.wait_ge(S("h_ready"), n0 + j + 1)
                if due(n0 + j):
                    pe.wait_ge(S("hT_copied"), n0 + j)
                for c in range(FC):
                    ins = pe.transpose(bank[2][:, P * c:P * c + P], hs[:, P * c:P * c + P], ident[:, :])
                ins.then_inc(S("hT_ps"), 1)

            def outputs(j):
                e = expert(pe, m, j)
                pe.wait_ge(S("hT_copied"), n0 + j + 1)
                if due(n0 + j):
                    pe.wait_ge(S("y_ready"), n0 + j)
                for c in range(FC):
                    ins = pe.matmul(bank[3][:, 0:D], hT[:, P * c:P * c + P], w2[:, bass.ds(e * F + P * c, D)],
                                    start=c == 0, stop=c == FC - 1)
                ins.then_inc(S("y_ps"), 1)

            def step(j, p, ok):
                if ok(-1):
                    transposes(j - 1)
                if ok(1):
                    tokens(j + 1, 1 - p)
                if ok(0):
                    hidden(j, p)
                if ok(-1):
                    outputs(j - 1)

            steps(pe, m.nb, -1, m.nb + 1, step)

        def act_blocks(act, m):
            n0 = m.before

            def hidden(j):
                if due(n0 + j):
                    act.wait_ge(S("hT_ps"), n0 + j)
                if m.kind == "gelu":
                    act.wait_ge(S("hb_ready"), j + 1)
                    ins = act.activation(hs[:, :], hb[:, :], ACT.Gelu_apprx_tanh)
                else:
                    act.wait_ge(S("h_ps"), n0 + j + 1)
                    ins = act.activation(hs[:, :], bank[1], ACT.Silu)
                ins.then_inc(S("h_ready"), 1)

            def outputs(j, p):
                act.wait_ge(S("y_ps"), n0 + j + 1)
                if due(m.stored(j, p)):
                    act.wait_ge(S(f"y_st{p}"), m.stored(j, p))
                act.activation(ys[:, p, :], bank[3][:, 0:D], ACT.Copy).then_inc(S("y_ready"), 1)

            def step(j, p, ok):
                if ok(0):
                    hidden(j)
                if ok(-1) and m.kind == "silu":
                    outputs(j - 1, 1 - p)

            steps(act, m.nb, -1, m.nb + 1, step)

        def dve_blocks(dve, link, m):
            n0 = m.before

            def copy_hT(j):
                dve.wait_ge(S("hT_ps"), n0 + j + 1)
                if due(n0 + j):
                    dve.wait_ge(S("y_ps"), n0 + j)
                if m.kind == "relu":
                    ins = dve.tensor_scalar(hT[:, :], bank[2], 0.0, None, ALU.max)
                else:
                    ins = dve.tensor_copy(hT[:, :], bank[2])
                ins.then_inc(S("hT_copied"), 1)

            def copy_xsT(j, p):
                dve.wait_ge(S("xsT_ps"), n0 + j + 1)
                if due(n0 + j - 1):
                    dve.wait_ge(S("h_ps"), n0 + j - 1)
                dve.tensor_copy(xsT[:, p, :], bank[0][:, 0:P]).then_inc(S("xsT_copied"), 1)

            def hidden(j):
                e = expert(dve, m, j)
                dve.wait_ge(S("h_ps"), n0 + j + 1)
                bias = b1r[:, bass.ds(e, 1), :].rearrange("p a f -> p (a f)")
                if m.kind == "gelu":
                    if due(n0 + j):
                        dve.wait_ge(S("h_ready"), n0 + j)
                    dve.tensor_tensor(hb[:, :], bank[1], bias, ALU.add).then_inc(S("hb_ready"), 1)
                else:
                    if due(n0 + j):
                        dve.wait_ge(S("hT_ps"), n0 + j)
                    dve.tensor_tensor(hs[:, :], bank[1], bias, ALU.add).then_inc(S("h_ready"), 1)

            def outputs(j, p):
                e = expert(dve, m, j)
                bias = b2r[:, m.layer // 2, bass.ds(e, 1), :].rearrange("p a d -> p (a d)")
                dve.wait_ge(S("y_ps"), n0 + j + 1)
                if m.kind == "gelu":
                    link(dve, dve.tensor_tensor(yb[:, :], bank[3][:, 0:D], bias, ALU.add))
                    if due(m.stored(j, p)):
                        dve.wait_ge(S(f"added{p}"), m.stored(j, p))
                    dve.tensor_scalar(ys[:, p, :], yb[:, :], rv[:, bass.ds(e, 1)], None, ALU.mult
                                      ).then_inc(S("y_ready"), 1)
                else:
                    if due(m.stored(j, p)):
                        dve.wait_ge(S(f"y_st{p}"), m.stored(j, p))
                    dve.tensor_tensor(ys[:, p, :], bank[3][:, 0:D], bias, ALU.add).then_inc(S("y_ready"), 1)

            def step(j, p, ok):
                if ok(-1):
                    copy_hT(j - 1)
                if ok(1):
                    copy_xsT(j + 1, 1 - p)
                if ok(0) and m.kind != "silu":
                    hidden(j)
                if ok(-1) and m.kind != "silu":
                    outputs(j - 1, 1 - p)

            steps(dve, m.nb, -1, m.nb + 1, step, link, int(m.kind == "gelu"))

        def sp_blocks(sp, m):
            n0 = m.before

            def load(j, p):
                if due(n0 + j - 1):
                    sp.wait_ge(S("xsT_ps"), n0 + j - 1)
                sp.dma_start(xs[:, p, :], xs_d[bass.ds(j * P, P), :]).then_inc(S(f"xs_ld{p}"), 16)

            def store(j, p):
                sp.wait_ge(S("y_ready"), n0 + j + 1)
                sp.dma_start(ys_d[bass.ds(j * P, P), :], ys[:, p, :]).then_inc(S(f"y_st{p}"), 16)

            def step(j, p, ok):
                if ok(0):
                    load(j, p)
                if ok(-4):
                    store(j - 4, p)

            sp.wait_ge(S("scattered"), 16 * B * (m.route + 1))
            for j in range(4):
                step(j, j % 2, lambda d, j=j: 0 <= j + d < m.nb)
            pairs = (m.nb - 4) // 2
            with sp.Fori(0, pairs) as t:
                for p in range(2):
                    step(4 + 2 * t + p, p, lambda d: True)
            for j in range(4 + 2 * pairs, m.nb + 4):
                step(j, j % 2, lambda d, j=j: 0 <= j + d < m.nb)

        def pe_logits(pe, k, router, E):
            for b in range(B):
                if b % 4 == 0:
                    pe.wait_ge(S("xnT_copied"), 2 * k.xt + b // 4 + 1)
                ins = pe.matmul(bank[4][:, E * b:E * b + E], xnT[:, P * b:P * b + P], router, start=True, stop=True)
            ins.then_inc(S("logits"), 1)

        def pe_counts(pe, k, E):
            pe.wait_ge(S("onehot"), k.route + 1)
            pe.matmul(bank[5][:, 0:B * E], tri[:, :], ohb[:, 0:B * E], start=True, stop=False)
            for b in range(B - 1):
                n = B - 1 - b
                pe.matmul(bank[5][:, E * b + E:B * E].rearrange("p (b e) -> p b e", b=n), onesb[:, :],
                          ohb[:, E * b:E * b + E].unsqueeze(1).to_broadcast([P, n, E]),
                          start=False, stop=b == B - 2)
            for b in range(B):
                ins = pe.matmul(bank[5][:, 256:256 + E], onesb[:, :], ohb[:, E * b:E * b + E],
                                start=b == 0, stop=b == B - 1)
            ins.then_inc(S("counts"), 1)

        def dve_softmax(dve, link, k, E, bias=None):
            v = lambda t: t[:, 0:B * E].rearrange("p (b e) -> p b e", b=B)
            dve.wait_ge(S("logits"), k.logits + 1)
            if bias is None:
                link(dve, dve.tensor_copy(lg[:, 0:B * E], bank[4][:, 0:B * E]))
            else:
                link(dve, dve.tensor_tensor(v(lg), v(bank[4]), bias.unsqueeze(1).to_broadcast([P, B, E]), ALU.add))
            link(dve, dve.tensor_reduce(r1[:, :].unsqueeze(2), v(lg), AX.X, ALU.max))
            dve.tensor_tensor(v(lg), v(lg), r1[:, :].unsqueeze(2).to_broadcast([P, B, E]), ALU.subtract
                              ).then_inc(S("logits_shifted"), 1)
            dve.wait_ge(S("logits_exp"), k.exps + 1)
            link(dve, dve.tensor_reduce(r1[:, :].unsqueeze(2), v(lt), AX.X, ALU.add))
            link(dve, dve.reciprocal(r1[:, :], r1[:, :]))
            return dve.tensor_tensor(v(lt), v(lt), r1[:, :].unsqueeze(2).to_broadcast([P, B, E]), ALU.mult)

        def act_softmax(act, k, E):
            act.wait_ge(S("logits_shifted"), k.exps + 1)
            act.activation(lt[:, 0:B * E], lg[:, 0:B * E], ACT.Exp).then_inc(S("logits_exp"), 1)

        def dve_route(dve, link, k, E, nb, src):
            v = lambda t: t[:, 0:B * E].rearrange("p (b e) -> p b e", b=B)
            wide = lambda t: t[:, :].unsqueeze(2).to_broadcast([P, B, E])
            over = lambda t: t[:, 0:E].unsqueeze(1).to_broadcast([P, B, E])
            link(dve, dve.tensor_reduce(wtop[:, :].unsqueeze(2), v(src), AX.X, ALU.max))
            link(dve, dve.tensor_tensor(v(lg), v(src), wide(wtop), ALU.is_equal))
            link(dve, dve.tensor_tensor(v(lg), v(lg), over(erev), ALU.mult))
            link(dve, dve.tensor_reduce(r1[:, :].unsqueeze(2), v(lg), AX.X, ALU.max))
            dve.tensor_tensor(v(ohb), v(lg), wide(r1), ALU.is_equal).then_inc(S("onehot"), 1)
            dve.wait_ge(S("counts"), k.route + 1)
            link(dve, dve.tensor_scalar(ci[:, 0:E], bank[5][:, 256:256 + E], float(P - 1), None, ALU.add))
            link(dve, dve.tensor_scalar(ci[:, 0:E], ci[:, 0:E], 7, None, ALU.arith_shift_right))
            link(dve, dve.tensor_copy(c1[:, 0:E], ci[:, 0:E]))
            link(dve, dve.tensor_tensor_scan(c2[:, 0:E], ones[:, 0:E], c1[:, 0:E], 0.0, ALU.mult, ALU.add))
            link(dve, dve.tensor_tensor(c1[:, 0:E], c2[:, 0:E], c1[:, 0:E], ALU.subtract))
            link(dve, dve.scalar_tensor_tensor(v(lg), over(c1), float(P), v(bank[5]), ALU.mult, ALU.add))
            link(dve, dve.tensor_tensor(v(lg), v(lg), v(ohb), ALU.mult))
            link(dve, dve.tensor_reduce(slotf[:, :].unsqueeze(2), v(lg), AX.X, ALU.add))
            dve.tensor_copy(slot[:, :], slotf[:, :]).then_inc(S("slots"), 1)
            link(dve, dve.tensor_tensor(jcmp[:, 0:nb, 0:E], c2[0:1, 0:E].unsqueeze(1).to_broadcast([1, nb, E]),
                                        jrow[:, 0:nb].unsqueeze(2).to_broadcast([1, nb, E]), ALU.is_le))
            link(dve, dve.tensor_reduce(bef[:, 0:nb].unsqueeze(2), jcmp[:, 0:nb, 0:E], AX.X, ALU.add))
            dve.tensor_scalar(be[:, 0:nb], bef[:, 0:nb], float(E - 1), None, ALU.min).then_inc(S("block_experts"), 1)

        def pool_scatter(pool, k, src):
            pool.wait_ge(S("slots_cleared"), 16)
            pool.wait_ge(S("slots"), k.route + 1)
            for b in range(B):
                pool.indirect_dma_start(xs_d[:, :], bass.IndirectOffsetOnAxis(slot[:, b:b + 1], 0), src[:, b, :], None
                                        ).then_inc(S("scattered"), 16)

        def pool_gather(pool, m):
            for p in range(2):
                pool.wait_ge(S(f"y_st{p}"), m.all_stored(p))
            for b in range(B):
                pool.indirect_dma_start(yg[:, b, :], None, ys_d[0:P * m.nb, :], bass.IndirectOffsetOnAxis(slot[:, b:b + 1], 0)
                                        ).then_inc(S("back"), 16)

        def pe_choice(pe):
            pe_xnT(pe, 1, "xn_ready", B)
            pe_logits(pe, M0, rw[:, 0, :], E8)
            pe.wait_ge(S("probs"), 1)
            for b in range(B):
                ins = pe.transpose(bank[6 + b // 4][0:E8, P * (b % 4):P * (b % 4) + P], lt[:, E8 * b:E8 * b + E8],
                                   ident[:, :])
            ins.then_inc(S("probsT"), 1)
            pe.wait_ge(S("chosen"), 1)
            for n in range(2):
                ins = pe.transpose(bank[4][:, E8 * n:E8 * n + E8], top[:, n, :], ident[0:E8, 0:E8])
            ins.then_inc(S("chosenT"), 1)
            pe_blocks(pe, M0)

        def dve_choice(dve, link):
            dve_softmax(dve, link, M0, E8, bs8[:, :]).then_inc(S("probs"), 1)
            dve.wait_ge(S("probsT"), 1)
            link(dve, dve.tensor_copy(work[:, :], psum[0:E8, 6:8, :].rearrange("p a n -> p (a n)")))
            for r in range(CAP // 8):
                t = slice(8 * r, 8 * r + 8)
                link(dve, dve.max(top[:, 0, t], work[:, :]))
                dve.max_index(topi[:, t], top[:, 0, t], work[:, :])
                link(dve, dve.match_replace(work[:, :], top[:, 0, t], work[:, :], -1.0))
            dve.tensor_copy(top[:, 1, :], topi[:, :]).then_inc(S("chosen"), 1)
            dve.wait_ge(S("chosenT"), 1)
            dve.tensor_copy(rv[:, :], bank[4][:, 0:E8])
            dve.tensor_copy(idx[:, :], bank[4][:, E8:2 * E8]).then_inc(S("indices"), 1)
            dve.wait_ge(S("indices"), 1)
            dve_blocks(dve, link, M0)

        def pool_choice(pool):
            def gather(j):
                p = j % 2
                if due(j - 1):
                    pool.wait_ge(S("xsT_ps"), j - 1)
                pool.indirect_dma_start(xs[:, p, :], None, xn_d[:, :], bass.IndirectOffsetOnAxis(idx[:, j:j + 1], 0)
                                        ).then_inc(S(f"gathered{p}"), 16)

            def scatter(j):
                p = j % 2
                pool.wait_ge(S("y_ready"), j + 1)
                if due(16 * ((j + 1) // 2)):
                    pool.wait_ge(S(f"added{1 - p}"), 16 * ((j + 1) // 2))
                pool.indirect_dma_start(acc_d[:, :], bass.IndirectOffsetOnAxis(idx[:, j:j + 1], 0), ys[:, p, :], None,
                                        compute_op=ALU.add).then_inc(S(f"added{p}"), 16)

            pool.wait_ge(S("indices"), 1)
            pool.wait_ge(S("xn_stored"), 16)
            pool.wait_ge(S("x_stored"), 16)
            for j in range(B + 2):
                if j < B:
                    gather(j)
                if j >= 2:
                    scatter(j - 2)

        def dve_quantised_weights(dve, link):
            v = wqr[:, :, :].rearrange("p n (k i) -> p (n k) i", i=32)
            wide = lambda t: t[:, :].unsqueeze(2).to_broadcast([P, 36, 32])
            flat = wqr[:, :, :].rearrange("p n k -> p (n k)")
            dve.wait_ge(S("ld_wqr"), 48)
            link(dve, dve.tensor_reduce(wsc[:, :].unsqueeze(2), v, AX.X, ALU.max, apply_absolute_value=True))
            link(dve, dve.tensor_scalar(wsc[:, :], wsc[:, :], 1.0 / WMAX, TINY, ALU.mult, ALU.max))
            link(dve, dve.reciprocal(wrc[:, :], wsc[:, :]))
            link(dve, dve.tensor_tensor(v, v, wide(wrc), ALU.mult))
            link(dve, dve.tensor_scalar(flat, flat, WMAX, -WMAX - 1.0, ALU.min, ALU.max))
            link(dve, dve.tensor_scalar(flat, flat, MAGIC, MAGIC, ALU.add, ALU.subtract))
            dve.tensor_tensor(v, v, wide(wsc), ALU.mult).then_inc(S("wq4"), 1)

        def pe_quantised_weights(pe):
            pe.wait_ge(S("wq4"), 1)
            for n in range(3):
                for t in range(QC):
                    ins = pe.transpose(bank[4 + n][:, P * t:P * t + P], wqr[:, n, P * t:P * t + P], ident[:, :])
                ins.then_inc(S("wq4T_ps"), 1)

        def act_quantised_weights(act):
            for n in range(3):
                act.wait_ge(S("wq4T_ps"), n + 1)
                act.activation(wqT[:, n, :], bank[4 + n][:, 0:QF], ACT.Copy).then_inc(S("wq4T"), 1)

        def dve_scale(dve, link, k, unit=None):
            dve.wait_ge(S("row_max_ps"), k + 1)
            dve.tensor_reduce(qrow[:, :], bank[7][0:1, 0:P], AX.X, ALU.max).then_inc(S("max_one"), 1)
            dve.wait_ge(S("max_all_ps"), k + 1)
            if unit is None:
                link(dve, dve.tensor_scalar(am[:, 6:7], bank[7][:, P:P + 1], 1.0, None, ALU.mult))
            else:
                link(dve, dve.tensor_scalar(am[:, 6:7], bank[7][:, P:P + 1], unit, None, ALU.mult))
            dst = qs[:, k, :] if k < 3 else qo[:, k - 3, :]
            link(dve, dve.tensor_scalar(dst[:, 0:1], am[:, 6:7], 1.0 / QMAX, TINY, ALU.mult, ALU.max))
            link(dve, dve.reciprocal(dst[:, 1:2], dst[:, 0:1]))
            if unit is not None:
                link(dve, dve.tensor_scalar(dst[:, 1:2], dst[:, 1:2], unit, None, ALU.mult))
            return dst

        def pe_scale(pe, k):
            pe.wait_ge(S("row_max"), k + 1)
            pe.transpose(bank[7][0:1, 0:P], am[:, 6:7], ident[:, :]).then_inc(S("row_max_ps"), 1)
            pe.wait_ge(S("max_one"), k + 1)
            pe.matmul(bank[7][:, P:P + 1], ones[0:1, :], qrow[:, :], start=True, stop=True
                      ).then_inc(S("max_all_ps"), 1)

        def dve_row_max(dve, t):
            dve.tensor_reduce(am[:, 6:7], t, AX.X, ALU.max, apply_absolute_value=True).then_inc(S("row_max"), 1)

        def to_integers(eng, link, t, r):
            link(eng, eng.tensor_scalar(t, t, r, QMAX, ALU.mult, ALU.min))
            link(eng, eng.tensor_scalar(t, t, -QMAX - 1.0, MAGIC, ALU.max, ALU.add))

        def dve_quantised(dve, link):
            flat = xn[:, :, :].rearrange("p b d -> p (b d)")
            dve.wait_ge(S("xn_ready"), 32)
            dve_row_max(dve, flat)
            q = dve_scale(dve, link, 0)
            to_integers(dve, link, flat, q[:, 1:2])
            dve.tensor_scalar(flat, flat, MAGIC, q[:, 0:1], ALU.subtract, ALU.mult).then_inc(S("xq_ready"), 1)
            for which, t in enumerate((QG, QU)):
                for n in range(6):
                    dve.wait_ge(S("gu_copied"), 6 * which + n + 1)
                    piece = t.rearrange("p (t n) -> p t n", t=QC)[:, n % 3, 512 * (n // 3):512 * (n // 3) + 512]
                    last = dve.tensor_reduce(am[:, n:n + 1], piece, AX.X, ALU.max, apply_absolute_value=True)
                link(dve, last)
                dve.tensor_reduce(am[:, 6:7], am[:, 0:6], AX.X, ALU.max).then_inc(S("row_max"), 1)
                q = dve_scale(dve, link, 1 + which)
                if which == 0:
                    to_integers(dve, link, QG, q[:, 1:2])
                    dve.tensor_scalar(QG, QG, MAGIC, q[:, 0:1], ALU.subtract, ALU.mult).then_inc(S("gate_q"), 1)
                else:
                    dve.engine_nop().then_inc(S("up_scale"), 1)
            dve.wait_ge(S("sigmoid"), 1)
            link(dve, dve.tensor_scalar(QV, QV, 65536.0, MAGIC, ALU.mult, ALU.add))
            link(dve, dve.tensor_scalar(QV, QV, MAGIC, MAGIC + 65535.0, ALU.max, ALU.min))
            link(dve, dve.scalar_tensor_tensor(QV, QV, MAGIC, QG, ALU.subtract, ALU.mult))
            dve_row_max(dve, QV)
            q = dve_scale(dve, link, 3, 2.0 ** -16)
            to_integers(dve, link, QV, q[:, 1:2])
            dve.wait_ge(S("up_q"), 1)
            link(dve, dve.scalar_tensor_tensor(QV, QV, MAGIC, QU, ALU.subtract, ALU.mult))
            dve_row_max(dve, QV)
            q = dve_scale(dve, link, 4, q[:, 0:1])
            to_integers(dve, link, QV, q[:, 1:2])
            dve.tensor_scalar(QV, QV, MAGIC, q[:, 0:1], ALU.subtract, ALU.mult).then_inc(S("o_q"), 1)
            for n in range(2):
                dve.wait_ge(S("down_ps"), n + 1)
                xv = x[:, 4 * n:4 * n + 4, :].rearrange("p b d -> p (b d)")
                dve.tensor_tensor(xv, xv, bank[n], ALU.add).then_inc(S("x_quantised"), 1)
            dve.wait_ge(S("x_quantised"), 2)

        def pool_quantised(pool, link):
            pool.wait_ge(S("up_scale"), 1)
            to_integers(pool, link, QU, qs[:, 2, 1:2])
            pool.tensor_scalar(QU, QU, MAGIC, qs[:, 2, 0:1], ALU.subtract, ALU.mult).then_inc(S("up_q"), 1)
            pool.wait_ge(S("b1_folded_ps"), E8)
            for e in range(E8):
                w = W1[2][:, F * e:F * e + F]
                pool.tensor_scalar(w, w, lnT[:, 0, e:e + 1], None, ALU.mult).then_inc(S("w1_folded"), 1)

        def act_quantised(act):
            for which, t in enumerate((QG, QU)):
                for n in range(6):
                    act.wait_ge(S("gu_ps"), 6 * which + n + 1)
                    piece = t.rearrange("p (t n) -> p t n", t=QC)[:, n % 3, 512 * (n // 3):512 * (n // 3) + 512]
                    act.activation(piece, bank[n], ACT.Copy).then_inc(S("gu_copied"), 1)
            act.wait_ge(S("gate_q"), 1)
            act.activation(QV, QG, ACT.Sigmoid).then_inc(S("sigmoid"), 1)
            for e in range(E8):
                act.wait_ge(S("b1_folded_ps"), e + 1)
                act.activation(b1r[:, e, :], bank[6], ACT.Copy).then_inc(S("b1_folded"), 1)

        def pe_quantised(pe):
            pe_scale(pe, 0)
            pe.wait_ge(S("xq_ready"), 1)
            pe_xnT(pe, 3, "xn_ready", 3 * B)
            pe.wait_ge(S("wq4T"), 3)
            pe.wait_ge(S("xnT_copied"), 8)
            for which in range(2):
                for n in range(6):
                    if which:
                        pe.wait_ge(S("gu_copied"), n + 1)
                    pe.matmul(bank[n], wqT[:, which, P * (n % 3):P * (n % 3) + P],
                              xnT[:, 512 * (n // 3):512 * (n // 3) + 512], start=True, stop=True
                              ).then_inc(S("gu_ps"), 1)
            pe_scale(pe, 1)
            pe_scale(pe, 2)
            for e in range(E8):
                if e:
                    if due(e):
                        pe.wait_ge(S("b1_folded"), e)
                w = slice(F * e, F * e + F)
                pe.matmul(bank[6], lnT[:, 1, e:e + 1].to_broadcast([P, P]), W1[2][:, w], start=True, stop=False)
                pe.matmul(bank[6], ident[0:E8, e:e + 1].to_broadcast([E8, P]), b8[:, :], start=False, stop=True
                          ).then_inc(S("b1_folded_ps"), 1)
            pe_scale(pe, 3)
            pe_scale(pe, 4)
            pe.wait_ge(S("o_q"), 1)
            for b in range(B):
                for c in range(QC):
                    ins = pe.matmul(bank[b // 4][:, P * (b % 4):P * (b % 4) + P],
                                    QV[:, B * P * c + P * b:B * P * c + P * b + P], wqT[:, 2, P * c:P * c + P],
                                    start=c == 0, stop=c == QC - 1)
                if b % 4 == 3:
                    ins.then_inc(S("down_ps"), 1)

        def dve_top(dve, link):
            dve.wait_ge(S("xn_ready"), 6 * B)
            dve_layernorm(dve, link, 6, xn, xn2)
            dve.wait_ge(S("logits"), M1.logits + 1)
            link(dve, dve.tensor_copy(lt[:, 0:B * E8], bank[4][:, 0:B * E8]))
            dve_route(dve, link, M1, E8, NB8, lt)
            dve_blocks(dve, link, M1)
            link(dve, dve.tensor_tensor(x[:, :, :], x[:, :, :], xn[:, :, :], ALU.add))
            dve.wait_ge(S("back"), 16 * B)
            link(dve, dve.tensor_tensor(x[:, :, :], x[:, :, :], yg, ALU.add))

        def pe_top(pe):
            pe_xnT(pe, 5, "xn_ready", 5 * B)
            pe_logits(pe, M1, rw[:, 1, :], E8)
            pe_counts(pe, M1, E8)
            pe.wait_ge(S("block_experts"), 1)
            pe.wait_ge(S("w1_folded"), E8)
            pe_blocks(pe, M1)

        def pool_top(pool, link):
            pool_rstd(pool, link, 6)
            pool.wait_ge(S("xn_ready"), 7 * B)
            pool_scatter(pool, M1, xn2)
            pool_gather(pool, M1)

        def dve_chain(dve, link, k):
            dve_softmax(dve, link, k, E16).then_inc(S("chain_probs"), 1)
            if due(k.exps):
                dve.wait_ge(S("chain_probs"), k.exps)
            dve_route(dve, link, k, E16, NB16, lt)
            dve_blocks(dve, link, k)
            dve.wait_ge(S("back"), 16 * B * (k.route + 1))
            w = wtop[:, :].unsqueeze(2).to_broadcast([P, B, D])
            if k is not MC[-1]:
                dve.tensor_tensor(xn[:, :, :], yg, w, ALU.mult).then_inc(S("chain_ready"), 1)
            else:
                link(dve, dve.tensor_tensor(yg, yg, w, ALU.mult))
                dve.tensor_tensor(x[:, :, :], x[:, :, :], yg, ALU.add).then_inc(S("x_final"), 1)

        def pe_chain(pe, k, i):
            if i == 0:
                pe.wait_ge(S("ld_rw16"), 16)
                pe_xnT(pe, k.xt, "xn_ready", 8 * B)
            else:
                pe_xnT(pe, k.xt, "chain_ready", i - 1, each=0)
            pe_logits(pe, k, rw16[:, i, :], E16)
            pe_counts(pe, k, E16)
            pe.wait_ge(S("block_experts"), k.route + 1)
            if i == 0:
                pe.wait_ge(S("ld_e3"), 16 * 17)
            pe_blocks(pe, k)

        block = ctx.enter_context(nc.Block())

        @block.sync
        def _(sp):
            row = lambda ap: ap.rearrange("(a n) -> a n", a=1)
            hdk = lambda ap: ap.rearrange("h d k -> d h k")
            sp.dma_start(craw, a["ctx_1024"].rearrange("b p d -> p b d")).then_inc(S("ld_ctx"), 16)
            for n, k in enumerate(["L0_xattn_Wq", "L0_xattn_Wk"]):
                sp.dma_start(wraw[:, n, :], a[k]).then_inc(S("ld_w"), 16)
            sp.dma_start(x[:, :, :], a["x"].rearrange("b p d -> p b d")).then_inc(S("ld_x"), 16)
            sp.dma_start(wv[:, 0, :], a["L0_xattn_Wv"]).then_inc(S("ld_wv"), 16)
            sp.dma_start(wo[:, 0, :], a["L0_xattn_Wo"]).then_inc(S("ld_wv"), 16)
            sp.dma_start(wraw[:, 2, :], a["L2_xattn_Wq"]).then_inc(S("ld_w"), 16)
            sp.dma_start(wraw[:, 3, :], a["L2_xattn_Wkv"][:, 0:D]).then_inc(S("ld_w"), 16)
            for n, k in ((4, "L3_xattn_Wq"), (5, "L3_xattn_Wk")):
                sp.dma_start(wraw[:, n, :].rearrange("p (h k) -> p h k", h=H), hdk(a[k])).then_inc(S("ld_w"), 16)
            for n, k in enumerate(["W_q", "W_k", "W_v", "W_proj"]):
                sp.dma_start(wraw[:, 6 + n, :], a["L1_xattn_" + k]).then_inc(S("ld_wt"), 16)
            for n, k in enumerate(["w_gate", "w_up"]):
                sp.dma_start(wqr[:, n, :].rearrange("p (t i) -> p t i", t=QC),
                             a["L1_ffn_" + k].rearrange("(t p) i -> p t i", p=P)).then_inc(S("ld_wqr"), 16)
            sp.dma_start(wqr[:, 2, :], a["L1_ffn_w_down"]).then_inc(S("ld_wqr"), 16)
            sp.dma_start(wv[:, 2, :], a["L2_xattn_Wkv"][:, D:2 * D]).then_inc(S("ld_wv"), 16)
            sp.dma_start(wv[:, 3, :].rearrange("p (h k) -> p h k", h=H), hdk(a["L3_xattn_Wv"])).then_inc(S("ld_wv"), 16)
            sp.dma_start(wo[:, 2, :], a["L2_xattn_Wo"]).then_inc(S("ld_wv"), 16)
            sp.dma_start(wo[:, 3, :], a["L3_xattn_Wo"]).then_inc(S("ld_wv"), 16)
            sp.wait_ge(S("brow_clear"), 2)
            hd = lambda ap: ap.rearrange("(a h d) -> a h d", a=1, d=DH)
            for n, ap in ((2, hd(a["L2_xattn_bq"])), (6, hd(a["L2_xattn_bkv"][0:D])),
                          (3, a["L3_xattn_bq"].rearrange("h (a d) -> a h d", a=1)),
                          (7, a["L3_xattn_bk"].rearrange("h (a d) -> a h d", a=1))):
                sp.dma_start(brow[0:1, n, :, 0:DH], ap).then_inc(S("ld_brow"), 16)
            sp.dma_start(bv[:, 0, :], row(a["L2_xattn_bkv"][D:2 * D]).to_broadcast([P, D])).then_inc(S("ld_bo"), 16)
            sp.dma_start(bv[:, 1, :], a["L3_xattn_bv"].rearrange("h (a d) -> a (h d)", a=1).to_broadcast([P, D])
                         ).then_inc(S("ld_bo"), 16)
            for n, k in enumerate(["L1_xattn_b_proj", "L2_xattn_bo", "L3_xattn_bo"]):
                sp.dma_start(bo[:, n, :], row(a[k]).to_broadcast([P, D])).then_inc(S("ld_bo"), 16)
            for L, name in ((0, "ld_e0"), (2, "ld_e2")):
                k = f"L{L}_ffn_"
                sp.dma_start(W1[L].rearrange("p (e f) -> p e f", e=E8), a[k + "W1"].rearrange("e d f -> d e f")
                             ).then_inc(S(name), 16)
                for e in range(E8):
                    sp.dma_start(W2[L][:, F * e:F * e + F].rearrange("p (c d) -> p c d", c=FC),
                                 a[k + "W2"][e].rearrange("(c p) d -> p c d", p=P)).then_inc(S(name), 16)
                sp.dma_start(b2r[:, L // 2, :, :].rearrange("p e d -> p (e d)"),
                             a[k + "b2"].rearrange("e (a d) -> a (e d)", a=1).to_broadcast([P, E8 * D])
                             ).then_inc(S(name), 16)
                if L == 0:
                    sp.dma_start(b1r[:, :, :].rearrange("p e f -> p (e f)"),
                                 a[k + "b1"].rearrange("e (a f) -> a (e f)", a=1).to_broadcast([P, E8 * F])
                                 ).then_inc(S(name), 16)
                    sp.dma_start(rw[:, 0, :], a[k + "Ws"]).then_inc(S(name), 16)
                    sp.dma_start(bs8[:, :], row(a[k + "bs"]).to_broadcast([P, E8])).then_inc(S(name), 16)
            sp.dma_start(b8[:, :], a["L2_ffn_b1"]).then_inc(S("ld_e8w"), 16)
            for n, k in enumerate(["ln_g", "ln_b", "centroids"]):
                sp.dma_start(e8w[:, n, :], a["L2_ffn_" + k]).then_inc(S("ld_e8w"), 16)
            sp.dma_start(rw16[:, :, :], a["L3_ffn_routers"].rearrange("n d e -> d n e")).then_inc(S("ld_rw16"), 16)
            sp.wait_ge(S("zero"), 1)
            sp.dma_start(xs_d.rearrange("(j p) d -> p j d", p=P), hT[:, 0:D].unsqueeze(1).to_broadcast([P, NB16, D])
                         ).then_inc(S("slots_cleared"), 16)
            sp.dma_start(mask8[:, :, :], a["mask_Bx1xSxS2_bk0"].rearrange("b a q k -> q (a b) k")
                         ).then_inc(S("ld_mask"), 16)
            sp.wait_ge(S("xn_ready"), 2 * B)
            sp.dma_start(xn_d.rearrange("(b p) d -> p b d", p=P), xn[:, :, :]).then_inc(S("xn_stored"), 16)
            sp.dma_start(acc_d.rearrange("(b p) d -> p b d", p=P), x[:, :, :]).then_inc(S("x_stored"), 16)
            for p in range(2):
                sp.wait_ge(S(f"added{p}"), 16 * B // 2)
            sp.dma_start(x[:, :, :], acc_d.rearrange("(b p) d -> p b d", p=P)).then_inc(S("x_back"), 16)
            sp.wait_ge(S("y_ready"), M0.nb)
            sp.dma_start(W1[3].rearrange("p (e f) -> p e f", e=E16), a["L3_ffn_W1"].rearrange("e d f -> d e f")
                         ).then_inc(S("ld_e3"), 16)
            sp_blocks(sp, M1)
            for e in range(E16):
                sp.dma_start(W2[3][:, F * e:F * e + F].rearrange("p (c d) -> p c d", c=FC),
                             a["L3_ffn_W2"][e].rearrange("(c p) d -> p c d", p=P)).then_inc(S("ld_e3"), 16)
            for k in MC:
                sp_blocks(sp, k)
            sp.wait_ge(S("x_final"), 1)
            sp.dma_start(out.rearrange("b p d -> p b d"), x[:, :, :]).then_inc(S("st_out"), 16)
            sp.wait_ge(S("st_out"), 16)

        @block.gpsimd
        def _(pool):
            link = Link(S("pool_step"))
            pool.memset(brow[:, :, :, :], 0.0).then_inc(S("brow_clear"), 1)
            pool.wait_ge(S("brow_clear"), 1)
            pool.memset(brow[:, 4:8, :, DH:DH + 1], 1.0).then_inc(S("brow_clear"), 1)
            pool.memset(ident[:, :], 0.0)
            pool.memset(tri[:, :], 1.0)
            pool.memset(ones[:, :], 1.0)
            pool.memset(onesb[:, :], 1.0)
            pool.memset(hmask[:, :], 1.0)
            pool.memset(half[:, :], -0.5)
            pool.memset(sel[:, :, :], 0.0)
            pool.memset(hT[:, :], 0.0).then_inc(S("zero"), 1)
            pool.memset(Mp[:, :, :], 0.0)
            pool.memset(Va[:, :, :, DH:DH + 1], 1.0)
            pool.memset(wq[:, :, :, :], 0.0)
            link(pool, pool.memset(wk[:, :, :, :], 0.0))
            pool.iota(iot[:, :], [[1, 24]], 0, 0)
            link(pool, pool.affine_select(out=tri[:, :], in_=tri[:, :], compare_op=ALU.is_gt, fill=0.0, base=0,
                                          pattern=[[1, P]], channel_multiplier=-1))
            link(pool, pool.affine_select(out=hmask[:, :], in_=hmask[:, :], compare_op=ALU.is_ge, fill=0.0, base=0,
                                          pattern=[[-ROWS, HC]], channel_multiplier=1))
            link(pool, pool.affine_select(out=ident[:, :], in_=ident[:, :], compare_op=ALU.not_equal, fill=1.0,
                                          base=0, pattern=[[-1, P]], channel_multiplier=1))
            link(pool, pool.affine_select(out=sel[:, :, :], in_=sel[:, :, :], compare_op=ALU.not_equal, fill=1.0,
                                          base=0, pattern=[[-32, 4], [-1, DH + 1]], channel_multiplier=1))
            link(pool, pool.affine_select(out=hmask[:, :], in_=hmask[:, :], compare_op=ALU.is_ge, fill=0.0,
                                          base=ROWS - 1, pattern=[[ROWS, HC]], channel_multiplier=-1))
            pool.tensor_copy(identb[:, :], ident[:, :]).then_inc(S("consts"), 1)
            pool.tensor_scalar(erev[:, :], iot[:, 0:E16], -1.0, float(E16), ALU.mult, ALU.add)
            link(pool, pool.tensor_copy(jrow[:, :], iot[0:1, :]))
            pool.wait_ge(S("ld_w"), 16 * len(PAD))
            for name, layer, n in PAD:
                dst = (wq if name == "wq" else wk)[:, layer, :, 0:DH]
                last = pool.tensor_copy(dst, wraw[:, n, :].rearrange("p (h d) -> p h d", h=H))
            last.then_inc(S("w_pad"), 1)
            for L in range(4):
                pool_rstd(pool, link, XL[L])
                pool_attention(pool, L)
                pool_rstd(pool, link, XL[L] + 1)
                if L == 0:
                    pool_choice(pool)
                if L == 1:
                    pool_quantised(pool, link)
                if L == 2:
                    pool_top(pool, link)
                if L == 3:
                    for k in MC:
                        pool_scatter(pool, k, xn)
                        pool_gather(pool, k)

        @block.scalar
        def _(act):
            for n in range(2):
                act.wait_ge(S("ctx_ps"), n + 1)
                act.activation(ctxT[:, 512 * n:512 * n + 512], bank[n], ACT.Copy).then_inc(S("ctx_copied"), 1)
            act.wait_ge(S("bcol_ps"), 1)
            act.activation(bcol[:, :, :].rearrange("p n c -> p (n c)"), bank[2][:, 0:16], ACT.Copy
                           ).then_inc(S("bcol_copied"), 1)
            act.wait_ge(S("e8w_ps"), 1)
            act.activation(lnT[:, :, :].rearrange("p n e -> p (n e)"), bank[7][:, 0:2 * E8], ACT.Copy)
            act.activation(rw[:, 1, :], bank[7][:, 2 * E8:3 * E8], ACT.Copy).then_inc(S("e8w_copied"), 1)
            act_quantised_weights(act)
            act.wait_ge(S("bcol_copied"), 1)
            for L in range(4):
                act_attention(act, L)
                act_xnT(act, 2 * L + 1)
                if L == 0:
                    act_softmax(act, M0, E8)
                    act_blocks(act, M0)
                if L == 1:
                    act_quantised(act)
                if L == 3:
                    for k in MC:
                        if k is not MC[0]:
                            act_xnT(act, k.xt)
                        act_softmax(act, k, E16)
                        act_blocks(act, k)

        @block.vector
        def _(dve):
            link = Link(S("dve_step"))
            dve.wait_ge(S("wt_ps"), 1)
            for n, dst in enumerate((wq[:, 1, :, 0:DH], wk[:, 1, :, 0:DH])):
                dve.tensor_copy(dst, bank[3][:, P * n:P * n + P].rearrange("p (h d) -> p h d", h=H))
            dve.tensor_copy(wv[:, 1, :], bank[3][:, 2 * P:3 * P])
            dve.tensor_copy(wo[:, 1, :], bank[3][:, 3 * P:4 * P]).then_inc(S("wt_copied"), 1)
            dve.wait_ge(S("ld_mask"), 16)
            dve.tensor_scalar(fill[:, :, :], mask8[:, :, :], 1.0, -FILL, ALU.subtract, ALU.mult
                              ).then_inc(S("fill_ready"), 1)
            dve_quantised_weights(dve, link)
            dve.wait_ge(S("ld_x"), 16)
            for L in range(4):
                dve_layernorm(dve, link, XL[L], x, xn)
                dve_attention(dve, link, L)
                dve_layernorm(dve, link, XL[L] + 1, x, xn)
                if L == 0:
                    dve.wait_ge(S("ld_e0"), 16 * 13)
                    dve_choice(dve, link)
                    dve.wait_ge(S("x_back"), 16)
                if L == 1:
                    dve_quantised(dve, link)
                if L == 2:
                    dve_top(dve, link)
                if L == 3:
                    for k in MC:
                        dve_chain(dve, link, k)

        @block.tensor
        def _(pe):
            pe.wait_ge(S("consts"), 1)
            pe.wait_ge(S("ld_ctx"), 16)
            for b in range(B):
                ins = pe.transpose(bank[b // 4][:, P * (b % 4):P * (b % 4) + P], craw[:, b, :], ident[:, :])
                if b % 4 == 3:
                    ins.then_inc(S("ctx_ps"), 1)
            pe.wait_ge(S("ld_wt"), 64)
            for n in range(4):
                ins = pe.transpose(bank[3][:, P * n:P * n + P], wraw[:, 6 + n, :], ident[:, :])
            ins.then_inc(S("wt_ps"), 1)
            pe.wait_ge(S("ld_e8w"), 64)
            for n in range(3):
                ins = pe.transpose(bank[7][:, E8 * n:E8 * n + E8], e8w[:, n, :], ident[0:E8, 0:E8])
            ins.then_inc(S("e8w_ps"), 1)
            pe.wait_ge(S("ld_brow"), 64)
            pe.wait_ge(S("brow_clear"), 2)
            for n in range(8):
                for c in range(2):
                    ins = pe.matmul(bank[2][:, 2 * n + c:2 * n + c + 1],
                                    brow[0:1, n, HC * c:HC * c + HC, :].rearrange("p h r -> p (h r)"),
                                    ones[0:1, 0:1], start=True, stop=True)
            ins.then_inc(S("bcol_ps"), 1)
            pe.wait_ge(S("ctx_copied"), 2)
            pe.wait_ge(S("w_pad"), 1)
            pe.wait_ge(S("wt_copied"), 1)
            pe.wait_ge(S("fill_ready"), 1)
            pe.wait_ge(S("ld_wv"), 96)
            pe.wait_ge(S("bcol_copied"), 1)
            pe.wait_ge(S("e8w_copied"), 1)
            pe.wait_ge(S("ld_e2"), 160)
            pe_quantised_weights(pe)
            pe.wait_ge(S("wq4T"), 3)
            for L in range(4):
                pe_attention(pe, L)
                if L == 0:
                    pe.wait_ge(S("ld_e0"), 16 * 12)
                    pe_choice(pe)
                if L == 1:
                    pe_quantised(pe)
                if L == 2:
                    pe_top(pe)
                if L == 3:
                    for i, k in enumerate(MC):
                        pe_chain(pe, k, i)


XL = [0, 2, 4, 7]
XT = [0, 2, 4, 6]
XR = [0, 16, 32, 56]

_OUT = (B, P, D)


def kernel(**inputs):
    import numpy as _np
    import concourse.bacc as _bacc
    from concourse.bass_utils import run_bass_kernel_spmd as _run

    nc = _bacc.Bacc("TRN2", target_bir_lowering=False, num_devices=1)
    arrays, args = {}, {}
    for name in inputs:
        v = _np.ascontiguousarray(inputs[name])
        arrays[f"in_{name}"] = v
        args[name] = nc.dram_tensor(f"in_{name}", v.shape, mybir.dt.from_np(v.dtype), kind="ExternalInput").ap()
    out = nc.dram_tensor("out_0", _OUT, F32, kind="ExternalOutput").ap()
    build(nc, args, out)
    r = _run(nc, [arrays], core_ids=[0])
    return r.results[0]["out_0"]
```

```python
import concourse.bass as bass
from concourse import mybir
from contextlib import ExitStack

F32 = mybir.dt.float32
BF16 = mybir.dt.bfloat16
I32 = mybir.dt.int32
U32 = mybir.dt.uint32
U8 = mybir.dt.uint8
ALU = mybir.AluOpType
ACT = mybir.ActivationFunctionType
AX = mybir.AxisListType

P = 128
B = 8
D = 128
H, DH = 16, 8
ROWS = 16
HC = 8
F = 512
FC = F // P
QF = 384
QC = QF // P
E8, E16 = 8, 16
NB8 = B + E8 - 1
NB16 = B + E16 - 1
CAP = 128
NT = 4
FILL = -(2.0 ** 100)
SCALE = float(DH) ** -0.5
EPS = 1e-5
MAGIC = 1.5 * 2.0 ** 23
QMAX = 32767.0
WMAX = 7.0
TINY = 1e-12


class Link:

    def __init__(self, sem):
        self.sem, self.n, self.turn = sem, 0, 0

    def __call__(self, eng, ins):
        ins.then_inc(self.sem, 1)
        self.n += 1
        eng.wait_ge(self.sem, self.turn + self.n)

    def enter(self, i, start, per):
        self.at, self.per, self.turn = self.n, per, (i - start) * per

    def leave(self, turns):
        assert self.n - self.at == self.per, (self.n - self.at, self.per)
        self.n, self.turn = self.at + self.per * turns, 0


class Mix:

    def __init__(self, layer, kind, E, nb, before, par, xt, logits, exps, route):
        self.layer, self.kind, self.E, self.nb = layer, kind, E, nb
        self.before, self.par = before, par
        self.xt, self.logits, self.exps, self.route = xt, logits, exps, route

    def stored(self, j, p):
        return 16 * self.par[p] + 8 * (j - p)

    def all_stored(self, p):
        return 16 * (self.par[p] + (self.nb + 1 - p) // 2)


M0 = Mix(0, "gelu", E8, B, 0, (0, 0), 1, 0, 0, None)
M1 = Mix(2, "relu", E8, NB8, B, (0, 0), 5, 1, 1, 0)
MC = [Mix(3, "silu", E16, NB16, B + NB8 + NB16 * i, ((NB8 + 1) // 2 + (NB16 + 1) // 2 * i, NB8 // 2 + NB16 // 2 * i),
          7 + i, 2 + i, 1 + i, 1 + i) for i in range(NT)]


def build(nc, a, out):
    ctx = ExitStack()
    with ctx:
        def sb(name, shape, dt=F32):
            return ctx.enter_context(nc.sbuf_tensor(name, shape, dt))

        sems = {}

        def S(name):
            if name not in sems:
                sems[name] = ctx.enter_context(nc.semaphore(name))
            return sems[name]

        def due(n):
            return not (isinstance(n, int) and n <= 0)

        x = sb("x", [P, B, D])
        xn = sb("xn", [P, B, D])
        xnT = sb("xnT", [P, B * P])
        ctxT = sb("ctxT", [P, B * P])
        KT = sb("KT", [P, 2, B, P])
        Va = sb("Va", [P, B, H, DH + 1])
        Qs = sb("Qs", [P, 2, P])
        Ks = sb("Ks", [P, 2, P])
        Qa = sb("Qa", [P, 2, P])
        Mp = sb("Mp", [P, H, ROWS])
        rs = sb("rs", [P, H])
        sel = sb("sel", [P, 4, DH + 1])
        o_sb = sb("o_sb", [P, D])
        oT = sb("oT", [P, P])
        scr = sb("scr", [P, 3 * QC * B * P])
        PT = scr[:, 0:2 * HC * P].rearrange("p (c n) -> p c n", c=2)
        QT = scr[:, 2048:4096].rearrange("p (c b q) -> p c b q", c=2, b=B)
        Km = scr[:, 4096:6144].rearrange("p (c j k) -> p c j k", c=2, j=HC)
        Qm = scr[:, 6144:8192].rearrange("p (c j q) -> p c j q", c=2, j=HC)
        ind = scr[:, 8192:9216].bitcast(BF16).rearrange("p (c n) -> p c n", c=2)
        wraw = scr[:, 7168:8448].rearrange("p (n d) -> p n d", n=10)
        work = scr[0:E8, 4096:5120]
        wqr = scr[:, 2048:3200].rearrange("p (n k) -> p n k", n=3)
        brow = scr[0:1, 4096:6144].rearrange("p (n h r) -> p n h r", n=8, h=H)
        craw = scr[:, 0:B * D].rearrange("p (b d) -> p b d", b=B)
        fill = sb("fill", [P, B, P], BF16)
        mask8 = sb("mask8", [P, B, P], U8)
        wq = sb("wq", [P, 4, H, ROWS])
        wk = sb("wk", [P, 4, H, ROWS])
        wv = sb("wv", [P, 4, D])
        wo = sb("wo", [P, 4, D])
        bcol = sb("bcol", [P, 8, 2])
        bv = sb("bv", [P, 2, D])
        bo = sb("bo", [P, 3, D])
        ident = sb("ident", [P, P])
        identb = sb("identb", [P, P], BF16)
        tri = sb("tri", [P, P], BF16)
        ones = sb("ones", [P, P])
        onesb = sb("onesb", [P, P], BF16)
        hmask = sb("hmask", [P, HC])
        half = sb("half", [P, B])
        spare = sb("spare", [P, 1])
        stats = sb("stats", [P, B, 6])
        mv = sb("mv", [P, B, 2])
        rstd = sb("rstd", [P, B])

        big = sb("big", [P, 4 * E8 * F])
        W1 = {0: big[:, 0:E8 * F], 2: big[:, 2 * E8 * F:3 * E8 * F], 3: big[:, 0:E16 * F]}
        W2 = {0: big[:, E8 * F:2 * E8 * F], 2: big[:, 3 * E8 * F:4 * E8 * F], 3: big[:, E16 * F:2 * E16 * F]}
        b1r = sb("b1r", [P, E8, F])
        b2r = sb("b2r", [P, 2, E8, D])
        lnT = sb("lnT", [P, 2, E8])
        b8 = sb("b8", [E8, F])
        e8w = sb("e8w", [E8, 3, D])
        rw = sb("rw", [P, 2, E8])
        rw16 = sb("rw16", [P, NT, E16])
        bs8 = sb("bs8", [P, E8])
        lg = sb("lg", [P, B * E16])
        lt = sb("lt", [P, B * E16])
        ohb = sb("ohb", [P, B * E16], BF16)
        r1 = sb("r1", [P, B])
        wtop = sb("wtop", [P, B])
        erev = sb("erev", [P, E16])
        c1 = sb("c1", [P, E16])
        c2 = sb("c2", [P, E16])
        ci = sb("ci", [P, E16], I32)
        slotf = sb("slotf", [P, B])
        slot = sb("slot", [P, B], I32)
        jrow = sb("jrow", [1, 24])
        iot = sb("iot", [P, 24], I32)
        jcmp = sb("jcmp", [1, 24, E16])
        bef = sb("bef", [1, 24])
        be = sb("be", [1, 24], I32)
        xs = sb("xs", [P, 2, D])
        xsT = sb("xsT", [P, 2, P])
        hb = sb("hb", [P, F])
        hs = sb("hs", [P, F])
        oU = hb
        Vs = hs[:, 0:H * (DH + 1)]
        hT = sb("hT", [P, F])
        ys = sb("ys", [P, 2, D])
        top = sb("top", [E8, 2, CAP])
        topi = sb("topi", [E8, CAP], U32)
        idx = sb("idx", [P, E8], I32)
        idxf = sb("idxf", [P, E8])
        rv = sb("rv", [P, E8])
        xn2 = scr[:, 2048:3072].rearrange("p (b d) -> p b d", b=B)
        yg = scr[:, 3072:4096].rearrange("p (b d) -> p b d", b=B)
        toki = scr[:, 0:B * P].bitcast(I32)
        tokf = scr[:, 1024:1024 + B * P]
        oh = scr[:, 2048:4096].rearrange("p (a t) -> p a t", a=2)
        W1s = scr[:, 4096:5120].rearrange("p (a f) -> p a f", a=2)
        xs_d = nc.dram_tensor("xs_d", (NB16 * P, D), F32, kind="Internal").ap()
        ys_d = nc.dram_tensor("ys_d", (NB16 * P, D), F32, kind="Internal").ap()
        xn_d = nc.dram_tensor("xn_d", (B * P, D), F32, kind="Internal").ap()

        wqT = sb("wqT", [P, 3, QF])
        wsc = sb("wsc", [P, 36])
        wrc = sb("wrc", [P, 36])
        am = sb("am", [P, 7])
        qrow = sb("qrow", [1, 1])
        qs = sb("qs", [P, 4, 2])
        qo = sb("qo", [P, 3, 2])
        QG, QU, QV = (scr[:, QC * B * P * n:QC * B * P * (n + 1)] for n in range(3))

        psum = ctx.enter_context(nc.psum_tensor("psum", [P, 8, 512], F32))
        bank = [psum[:, n, :] for n in range(8)]

        Qmf = [Qm[:, c, :, :].rearrange("p j q -> p (j q)") for c in range(2)]
        Kmf = [Km[:, c, :, :].rearrange("p j q -> p (j q)") for c in range(2)]
        Mpf = Mp[:, :, :].rearrange("p h r -> p (h r)")
        avs = bank[6][:, 0:H * (DH + 1)].rearrange("p (h n) -> p h n", h=H)
        VB = {2: 0, 3: 1}
        OB = {1: 0, 2: 1, 3: 2}
        PAD = [("wq", 0, 0), ("wk", 0, 1), ("wq", 2, 2), ("wk", 2, 3), ("wq", 3, 4), ("wk", 3, 5)]

        def pool_rstd(pool, link, n):
            pool.wait_ge(S("var_ready"), n + 1)
            link(pool, pool.tensor_scalar(rstd[:, :], mv[:, :, 1], EPS, None, ALU.add))
            pool.tensor_tensor(rstd[:, :], rstd[:, :], half[:, :], ALU.pow).then_inc(S("rstd_ready"), 1)

        def pool_attention(pool, L):
            n0 = B * L

            def values(i):
                if due(n0 + i):
                    pool.wait_ge(S("av1"), n0 + i)
                pool.tensor_copy(Vs, Va[:, bass.ds(i, 1), :, :].rearrange("p a h n -> p (a h n)")
                                 ).then_inc(S("vs_ready"), 1)

            def masked_keys(i):
                for c in range(2):
                    if due(n0 + i):
                        pool.wait_ge(S(f"scores{c}"), n0 + i)
                    pool.tensor_tensor(Km[:, c, :, :], KT[:, c, bass.ds(i, 1), :].to_broadcast([P, HC, P]),
                                       hmask[:, :].unsqueeze(2).to_broadcast([P, HC, P]), ALU.mult
                                       ).then_inc(S(f"km_ready{c}"), 1)

            pool.wait_ge(S("k_copied"), 4 * L + 4)
            pool.wait_ge(S("q_copied"), 4 * L + 4)
            masked_keys(0)
            pool.wait_ge(S("v_copied"), L + 1)
            values(0)
            masked_keys(1)
            with pool.Fori(1, B - 1) as i:
                masked_keys(i + 1)
                values(i)
            values(B - 1)

        def act_xnT(act, m):
            for n in range(2):
                act.wait_ge(S("xnT_ps"), 2 * m + n + 1)
                act.activation(xnT[:, 512 * n:512 * n + 512], bank[n], ACT.Copy).then_inc(S("xnT_copied"), 1)

        def act_attention(act, L):
            n0 = B * L

            def copies(dst, src_sem, done, row):
                for n in range(4):
                    h, c = n // 2, n % 2
                    act.wait_ge(S(src_sem), 4 * L + n + 1)
                    act.activation(dst[:, c, 4 * h:4 * h + 4, :].rearrange("p b k -> p (b k)"), bank[4 + n],
                                   ACT.Identity, bias=bcol[:, row, c:c + 1]).then_inc(S(done), 1)

            def exp(i, c):
                act.wait_ge(S(f"weights_ps{c}"), n0 + i + 1)
                if due(n0 + i):
                    act.wait_ge(S(f"av{c}"), n0 + i)
                act.activation(PT[:, c, :], psum[:, 4:6, :].rearrange("p a n -> p (a n)"), ACT.Exp, scale=SCALE
                               ).then_inc(S(f"exp{c}"), 1)

            def copy_oT(i):
                act.wait_ge(S("oT_ps"), n0 + i + 1)
                if due(n0 + i):
                    act.wait_ge(S("proj_ps"), n0 + i)
                act.activation(oT[:, :], bank[6][:, 256:384], ACT.Copy).then_inc(S("oT_copied"), 1)

            def copy_oU(i):
                act.wait_ge(S("av1"), n0 + i + 1)
                if due(n0 + i):
                    act.wait_ge(S("avs_ps"), n0 + i)
                act.activation(oU[:, :], bank[7], ACT.Copy).then_inc(S("oU_copied"), 1)

            copies(KT, "k_ps", "k_copied", 4 + L)
            if L == 0:
                act.wait_ge(S("e8w_ps"), 1)
                act.activation(lnT[:, :, :].rearrange("p n e -> p (n e)"), bank[0][:, 0:2 * E8], ACT.Copy)
                act.activation(rw[:, 1, :], bank[0][:, 2 * E8:3 * E8], ACT.Copy).then_inc(S("e8w_copied"), 1)
                act_quantised_weights(act)
            act_xnT(act, XT[L])
            copies(QT, "q_ps", "q_copied", L)
            def take_queries(i):
                if due(n0 + i):
                    act.wait_ge(S("scores1"), n0 + i)
                act.activation(Qs[:, :, :], QT[:, :, bass.ds(i, 1), :].rearrange("p c a k -> p c (a k)"), ACT.Copy
                               ).then_inc(S("qs_ready"), 1)

            def take_keys(i):
                if due(n0 + i):
                    act.wait_ge(S("weights_ps1"), n0 + i)
                act.activation(Ks[:, :, :], KT[:, :, bass.ds(i, 1), :].rearrange("p c a k -> p c (a k)"), ACT.Copy
                               ).then_inc(S("ks_ready"), 1)

            def body(i, left=B):
                if left < B:
                    copy_oU(i - 1)
                exp(i, 0)
                if left < B:
                    copy_oT(i - 1)
                if left > 2:
                    take_queries(i + 2)
                exp(i, 1)
                if left > 1:
                    take_keys(i + 1)

            act.wait_ge(S("q_copied"), 4 * L + 4)
            take_queries(0)
            take_keys(0)
            take_queries(1)
            body(0)
            with act.Fori(1, B - 2) as i:
                body(i, 3)
            body(B - 2, 2)
            body(B - 1, 1)
            copy_oU(B - 1)
            copy_oT(B - 1)

        def dve_layernorm(dve, link, n, src, dst):
            for b in range(B):
                last = dve.bn_stats(stats[:, b, :], src[:, b, :])
            link(dve, last)
            for b in range(B):
                last = dve.bn_aggr(mv[:, b, :], stats[:, b, :])
            last.then_inc(S("var_ready"), 1)
            dve.wait_ge(S("rstd_ready"), n + 1)
            for b in range(B):
                dve.tensor_scalar(dst[:, b, :], src[:, b, :], mv[:, b, 0:1], rstd[:, b:b + 1],
                                  ALU.subtract, ALU.mult).then_inc(S("xn_ready"), 1)

        def dve_attention(dve, link, L):
            n0 = B * L

            def values():
                if L > 0:
                    dve.wait_ge(S("ld_bo"), 16 * 5)
                for n in range(2):
                    dve.wait_ge(S("v_ps"), 2 * L + n + 1)
                    src = bank[2 + n].rearrange("p (b h d) -> p b h d", b=4, h=H)
                    dst = Va[:, 4 * n:4 * n + 4, :, 0:DH]
                    if L in VB:
                        for b in range(4):
                            last = dve.tensor_tensor(dst[:, b], src[:, b],
                                                     bv[:, VB[L], :].rearrange("p (h d) -> p h d", h=H), ALU.add)
                    else:
                        last = dve.tensor_copy(dst, src)
                last.then_inc(S("v_copied"), 1)
                if L == 0:
                    dve.wait_ge(S("wt_ps"), 1)
                    for n, dst in enumerate((wq[:, 1, :, 0:DH], wk[:, 1, :, 0:DH])):
                        dve.tensor_copy(dst, bank[4][:, P * n:P * n + P].rearrange("p (h d) -> p h d", h=H))
                    dve.tensor_copy(wv[:, 1, :], bank[4][:, 2 * P:3 * P])
                    dve.tensor_copy(wo[:, 1, :], bank[4][:, 3 * P:4 * P]).then_inc(S("wt_copied"), 1)
                    dve.wait_ge(S("ld_mask"), 16)
                    dve.tensor_scalar(fill[:, :, :], mask8[:, :, :], 1.0, -FILL, ALU.subtract, ALU.mult
                                      ).then_inc(S("fill_ready"), 1)
                dve.wait_ge(S("q_copied"), 4 * L + 4)
                dve.memset(bank[7], 0.0).then_inc(S("bank7_clear"), 1)

            def masked_queries(i):
                dve.wait_ge(S("max_ps"), n0 + i + 1)
                link(dve, dve.tensor_tensor(Qa[:, :, :], bank[4][:, 0:256].rearrange("p (c q) -> p c q", c=2),
                                            QT[:, :, bass.ds(i, 1), :].rearrange("p c a q -> p c (a q)"), ALU.add))
                if due(n0 + i):
                    dve.wait_ge(S("weights_ps1"), n0 + i)
                for c in range(2):
                    dve.tensor_tensor(Qm[:, c, :, :], Qa[:, c, :].unsqueeze(1).to_broadcast([P, HC, P]),
                                      hmask[:, :].unsqueeze(2).to_broadcast([P, HC, P]), ALU.mult
                                      ).then_inc(S("qm_ready"), 1)

            def normalise(i):
                dve.wait_ge(S("avs_ps"), n0 + i + 1)
                link(dve, dve.reciprocal(rs[:, :].unsqueeze(2), avs[:, :, DH:DH + 1]))
                if due(n0 + i):
                    dve.wait_ge(S("oT_ps"), n0 + i)
                dve.tensor_tensor(o_sb[:, :].rearrange("p (h d) -> p h d", h=H), avs[:, :, 0:DH],
                                  rs[:, :].unsqueeze(2).to_broadcast([P, H, DH]), ALU.mult
                                  ).then_inc(S("o_ready"), 1)

            def raw(c):
                return psum[:, 2 * c:2 * c + 2, :]

            def zeros(i, c):
                dve.wait_ge(S(f"scores{c}"), n0 + i + 1)
                if due(n0 + i):
                    dve.wait_ge(S(f"weights_ps{c}"), n0 + i)
                dve.tensor_scalar(ind[:, c, :], raw(c).rearrange("p a n -> p (a n)"), 0.0, FILL,
                                  ALU.is_equal, ALU.mult).then_inc(S(f"zeros{c}"), 1)

            def maxima(i, c):
                if L == 0:
                    dve.wait_ge(S(f"masked{c}"), i + 1)
                else:
                    dve.wait_ge(S(f"scores{c}"), n0 + i + 1)
                if due(n0 + i):
                    dve.wait_ge(S("max_ps"), n0 + i)
                dve.tensor_reduce(Mp[:, HC * c:HC * c + HC, DH:DH + 1],
                                  raw(c).rearrange("p a (j k) -> p (a j) k", j=4), AX.X, ALU.max, negate=True
                                  ).then_inc(S(f"max{c}"), 1)

            def residual(i):
                dve.wait_ge(S("proj_ps"), n0 + i + 1)
                xi = x[:, bass.ds(i, 1), :].rearrange("p a d -> p (a d)")
                ins = dve.tensor_tensor(xi, xi, bank[6][:, 384:512], ALU.add)
                if L in OB:
                    link(dve, ins)
                    ins = dve.tensor_tensor(xi, xi, bo[:, OB[L], :], ALU.add)
                ins.then_inc(S("x_res"), 1)

            values()
            for c in range(2):
                if L == 0:
                    zeros(0, c)
                maxima(0, c)

            def body(i, first=False, last=False):
                masked_queries(i)
                if L > 0 and not last:
                    maxima(i + 1, 0)
                if not first:
                    normalise(i - 1)
                if not last:
                    if L == 0:
                        zeros(i + 1, 0)
                        maxima(i + 1, 0)
                        zeros(i + 1, 1)
                    maxima(i + 1, 1)
                if not first:
                    residual(i - 1)

            body(0, first=True)
            with dve.Fori(1, B - 1) as i:
                link.enter(i, 1, 2 + (L in OB))
                body(i)
                link.leave(B - 2)
            body(B - 1, last=True)
            normalise(B - 1)
            residual(B - 1)
            dve.wait_ge(S("x_res"), n0 + B)

        def pe_xnT(pe, m, ready, n):
            for b in range(B):
                pe.wait_ge(S(ready), n + b + 1)
                ins = pe.transpose(bank[b // 4][:, P * (b % 4):P * (b % 4) + P], xn[:, b, :], ident[:, :])
                if b % 4 == 3:
                    ins.then_inc(S("xnT_ps"), 1)

        def pe_attention(pe, L):
            n0 = B * L
            if L == 1:
                pe.wait_ge(S("ld_wv"), 64)
                pe.wait_ge(S("fill_ready"), 1)
                pe.wait_ge(S("w_pad"), len(PAD))
                pe.wait_ge(S("x_combined"), 1)
            if L == 2:
                pe.wait_ge(S("x_quantised"), 2)
                pe.wait_ge(S("b1_folded"), E8)
            if L == 3:
                pe.wait_ge(S("y_ready"), M0.nb + M1.nb)

            def project(w, src, n):
                h, c = n // 2, n % 2
                return pe.matmul(bank[4 + n], w[:, L, HC * c:HC * c + HC, :].rearrange("p h r -> p (h r)"),
                                 src[:, 512 * h:512 * h + 512], start=True, stop=True)

            def scores(i, c):
                pe.wait_ge(S("qs_ready"), n0 + i + 1)
                pe.wait_ge(S(f"km_ready{c}"), n0 + i + 1)
                if due(n0 + i):
                    pe.wait_ge(S(f"max{c}"), n0 + i)
                for r in range(2):
                    ins = pe.matmul(bank[2 * c + r], Qs[:, c, :], Kmf[c][:, 512 * r:512 * r + 512], start=True, stop=L > 1,
                                    skip_group_check=L < 2)
                if L == 1:
                    for r in range(2):
                        ins = pe.matmul(bank[2 * c + r].rearrange("p (j k) -> p j k", j=4), identb[:, :],
                                        fill[:, bass.ds(i, 1), :].to_broadcast([P, 4, P]),
                                        start=False, stop=True, skip_group_check=True)
                ins.then_inc(S(f"scores{c}"), 1)

            def mask_zeros(i, c):
                pe.wait_ge(S(f"zeros{c}"), i + 1)
                for r in range(2):
                    ins = pe.matmul(bank[2 * c + r], identb[:, :], ind[:, c, 512 * r:512 * r + 512],
                                    start=False, stop=True, skip_group_check=True)
                ins.then_inc(S(f"masked{c}"), 1)

            def maxima(i):
                pe.wait_ge(S("max0"), n0 + i + 1)
                pe.wait_ge(S("max1"), n0 + i + 1)
                if due(n0 + i):
                    pe.wait_ge(S("exp1"), n0 + i)
                for c in range(2):
                    ins = pe.transpose(bank[4][:, P * c:P * c + P], Mpf[:, P * c:P * c + P], ident[:, :])
                ins.then_inc(S("max_ps"), 1)

            def weights(i, c):
                pe.wait_ge(S("qm_ready"), 2 * (n0 + i) + c + 1)
                if c == 0:
                    pe.wait_ge(S("ks_ready"), n0 + i + 1)
                    if due(n0 + i):
                        pe.wait_ge(S("exp1"), n0 + i)
                else:
                    pe.wait_ge(S("exp0"), n0 + i + 1)
                for r in range(2):
                    ins = pe.matmul(bank[4 + r], Ks[:, c, :], Qmf[c][:, 512 * r:512 * r + 512], start=True, stop=L > 1,
                                    skip_group_check=L < 2)
                for r in range(2):
                    if L == 0:
                        for j in range(4):
                            k = P * (4 * r + j)
                            ins = pe.matmul(bank[4 + r][:, P * j:P * j + P], ind[:, c, k:k + P], identb[:, :],
                                            start=False, stop=True, skip_group_check=True)
                    if L == 1:
                        ins = pe.matmul(bank[4 + r].rearrange("p (j k) -> p j k", j=4),
                                        fill[:, bass.ds(i, 1), :].rearrange("p a k -> p (a k)"),
                                        identb[:, :].unsqueeze(1).to_broadcast([P, 4, P]),
                                        start=False, stop=True, skip_group_check=True)
                ins.then_inc(S(f"weights_ps{c}"), 1)

            def attend(i, c):
                pe.wait_ge(S(f"exp{c}"), n0 + i + 1)
                if c == 0:
                    pe.wait_ge(S("vs_ready"), n0 + i + 1)
                    if due(n0 + i):
                        pe.wait_ge(S("oU_copied"), n0 + i)
                for h in range(HC):
                    g, j = (HC * c + h) // 4, h % 4
                    v = (DH + 1) * (HC * c + h)
                    ins = pe.matmul(bank[7][32 * j:32 * j + DH + 1, P * g:P * g + P], Vs[:, v:v + DH + 1],
                                    PT[:, c, P * h:P * h + P], start=True, stop=True)
                ins.then_inc(S(f"av{c}"), 1)

            def turn_outputs(i):
                pe.wait_ge(S("oU_copied"), n0 + i + 1)
                if due(n0 + i):
                    pe.wait_ge(S("x_res"), n0 + i)
                for g in range(4):
                    w = 4 * (DH + 1)
                    ins = pe.matmul(bank[6][:, w * g:w * g + w], oU[:, P * g:P * g + P],
                                    sel[:, :, :].rearrange("p j n -> p (j n)"), start=True, stop=True)
                ins.then_inc(S("avs_ps"), 1)

            def out_transpose(i):
                pe.wait_ge(S("o_ready"), n0 + i + 1)
                pe.transpose(bank[6][:, 256:384], o_sb[:, :], ident[:, :]).then_inc(S("oT_ps"), 1)

            def out_project(i):
                pe.wait_ge(S("oT_copied"), n0 + i + 1)
                pe.matmul(bank[6][:, 384:512], oT[:, :], wo[:, L, :], start=True, stop=True
                          ).then_inc(S("proj_ps"), 1)

            for n in range(4):
                project(wk, ctxT, n).then_inc(S("k_ps"), 1)
            for b in range(B):
                ins = pe.matmul(bank[2 + b // 4][:, P * (b % 4):P * (b % 4) + P], ctxT[:, P * b:P * b + P],
                                wv[:, L, :], start=True, stop=True)
                if b % 4 == 3:
                    ins.then_inc(S("v_ps"), 1)
            if L == 0:
                pe.wait_ge(S("k_copied"), 4)
                pe.wait_ge(S("ld_wt"), 64)
                for n in range(4):
                    ins = pe.transpose(bank[4][:, P * n:P * n + P], wraw[:, 6 + n, :], ident[:, :])
                ins.then_inc(S("wt_ps"), 1)
                pe.wait_ge(S("ld_e8w"), 48)
                for n in range(3):
                    ins = pe.transpose(bank[0][:, E8 * n:E8 * n + E8], e8w[:, n, :], ident[0:E8, 0:E8])
                ins.then_inc(S("e8w_ps"), 1)
                pe_quantised_weights(pe)
                pe.wait_ge(S("e8w_copied"), 1)
                pe.wait_ge(S("wt_copied"), 1)
                pe.wait_ge(S("wq4T"), 3)
            pe_xnT(pe, XT[L], "xn_ready", XR[L])
            for n in range(4):
                pe.wait_ge(S("xnT_copied"), 2 * XT[L] + n // 2 + 1)
                pe.wait_ge(S("k_copied"), 4 * L + n + 1)
                project(wq, xnT, n).then_inc(S("q_ps"), 1)
            pe.wait_ge(S("bank7_clear"), L + 1)

            def body(i, first=False, last=False):
                if L > 0 and not first:
                    attend(i - 1, 0)
                maxima(i)
                if not first:
                    attend(i - 1, 1)
                if not last:
                    scores(i + 1, 0)
                weights(i, 0)
                if not first:
                    turn_outputs(i - 1)
                if L > 0 and not last:
                    scores(i + 1, 1)
                if not first:
                    out_transpose(i - 1)
                weights(i, 1)
                if L == 0:
                    if not last:
                        mask_zeros(i + 1, 0)
                        scores(i + 1, 1)
                    attend(i, 0)
                    if not last:
                        mask_zeros(i + 1, 1)
                if not first:
                    out_project(i - 1)

            for c in range(2):
                scores(0, c)
            if L == 0:
                for c in range(2):
                    mask_zeros(0, c)
            body(0, first=True)
            with pe.Fori(1, B - 1) as i:
                body(i)
            body(B - 1, last=True)
            if L > 0:
                attend(B - 1, 0)
            attend(B - 1, 1)
            turn_outputs(B - 1)
            out_transpose(B - 1)
            out_project(B - 1)

        def steps(eng, nb, first, last, step):
            turns = (nb - 3) // 4
            for j in range(first, 2):
                step(j, j % 2, lambda d, j=j: 0 <= j + d < nb)
            with eng.Fori(0, turns) as t:
                for p in range(4):
                    step(2 + 4 * t + p, p % 2, lambda d: True)
            for j in range(2 + 4 * turns, last):
                step(j, j % 2, lambda d, j=j: 0 <= j + d < nb)

        def expert(eng, m, j):
            if m.kind == "gelu":
                return j
            return eng.value_load(be[0:1, bass.ds(j, 1)], min_val=0, max_val=m.E - 1)

        def pe_blocks(pe, m):
            n0 = m.before
            w1, w2 = W1[m.layer], W2[m.layer]

            def tokens(j, p):
                pe.wait_ge(S(f"gathered{p}" if m.kind == "gelu" else f"xs_ld{p}"), m.stored(j, p) + 16)
                if due(n0 + j):
                    pe.wait_ge(S("xsT_copied"), n0 + j)
                pe.transpose(bank[0][:, 0:P], xs[:, p, :], ident[:, :]).then_inc(S("xsT_ps"), 1)

            def hidden_turned(j, p):
                pe.wait_ge(S("w1_staged"), n0 - MC[0].before + j + 1)
                pe.wait_ge(S("xsT_copied"), n0 + j + 1)
                pe.wait_ge(S("h_ready"), n0 + j - 1)
                for c in range(FC):
                    ins = pe.matmul(bank[1 + p][:, P * c:P * c + P], W1s[:, p, P * c:P * c + P], xsT[:, p, :],
                                    start=True, stop=True)
                ins.then_inc(S("h_ps"), 1)

            def hidden(j, p):
                e = expert(pe, m, j)
                pe.wait_ge(S("xsT_copied"), n0 + j + 1)
                pe.matmul(bank[1], xsT[:, p, :], w1[:, bass.ds(e * F, F)], start=True, stop=True
                          ).then_inc(S("h_ps"), 1)

            def transposes(j):
                pe.wait_ge(S("h_ready"), n0 + j + 1)
                if due(n0 + j):
                    pe.wait_ge(S("hT_copied"), n0 + j)
                for c in range(FC):
                    ins = pe.transpose(bank[2][:, P * c:P * c + P], hs[:, P * c:P * c + P], ident[:, :])
                ins.then_inc(S("hT_ps"), 1)

            def combine(j, p):
                pe.wait_ge(S("y_ready"), n0 + j + 1)
                for b in range(B):
                    ins = pe.matmul(bank[6 + b // 4][:, P * (b % 4):P * (b % 4) + P], oh[:, p, P * b:P * b + P],
                                    ys[:, p, :], start=False, stop=True, skip_group_check=True)
                ins.then_inc(S("combined"), 1)

            def outputs(j, p):
                e = expert(pe, m, j)
                rows = [hs, hT][p] if m.kind == "silu" else hT
                pe.wait_ge(S("h_ready" if m.kind == "silu" else "hT_copied"), n0 + j + 1)
                if due(n0 + j):
                    pe.wait_ge(S("y_ready"), n0 + j)
                for c in range(FC):
                    ins = pe.matmul(bank[3][:, 0:D], rows[:, P * c:P * c + P], w2[:, bass.ds(e * F + P * c, D)],
                                    start=c == 0, stop=c == FC - 1)
                ins.then_inc(S("y_ps"), 1)

            def step(j, p, ok):
                if m.kind == "silu":
                    if ok(0):
                        hidden_turned(j, p)
                    if ok(1):
                        tokens(j + 1, 1 - p)
                    if ok(-1):
                        outputs(j - 1, 1 - p)
                    return
                if ok(-1):
                    transposes(j - 1)
                if ok(1):
                    tokens(j + 1, 1 - p)
                if ok(0):
                    hidden(j, p)
                if ok(-1):
                    outputs(j - 1, 1 - p)
                if ok(-2) and m.kind == "gelu":
                    combine(j - 2, p)

            steps(pe, m.nb, -1, m.nb + (2 if m.kind == "gelu" else 1), step)

        def act_blocks(act, m):
            n0 = m.before

            def hidden(j, p):
                if m.kind == "gelu":
                    if due(n0 + j):
                        act.wait_ge(S("hT_ps"), n0 + j)
                    act.wait_ge(S("hb_ready"), j + 1)
                    ins = act.activation(hs[:, :], hb[:, :], ACT.Gelu_apprx_tanh)
                else:
                    act.wait_ge(S("h_ps"), n0 + j + 1)
                    act.wait_ge(S("y_ps"), n0 + j - 1)
                    ins = act.activation([hs, hT][p][:, :], bank[1 + p], ACT.Silu)
                ins.then_inc(S("h_ready"), 1)

            def outputs(j, p):
                act.wait_ge(S("y_ps"), n0 + j + 1)
                if due(m.stored(j, p)):
                    act.wait_ge(S(f"y_st{p}"), m.stored(j, p))
                act.activation(ys[:, p, :], bank[3][:, 0:D], ACT.Copy).then_inc(S("y_ready"), 1)

            def step(j, p, ok):
                if ok(0):
                    hidden(j, p)
                if ok(-1) and m.kind == "silu":
                    outputs(j - 1, 1 - p)

            steps(act, m.nb, -1, m.nb + 1, step)

        def dve_blocks(dve, link, m):
            n0 = m.before

            def copy_hT(j):
                dve.wait_ge(S("hT_ps"), n0 + j + 1)
                if due(n0 + j):
                    dve.wait_ge(S("y_ps"), n0 + j)
                if m.kind == "relu":
                    ins = dve.tensor_scalar(hT[:, :], bank[2], 0.0, None, ALU.max)
                else:
                    ins = dve.tensor_copy(hT[:, :], bank[2])
                ins.then_inc(S("hT_copied"), 1)

            def copy_xsT(j, p):
                dve.wait_ge(S("xsT_ps"), n0 + j + 1)
                if due(n0 + j - 1):
                    dve.wait_ge(S("h_ps"), n0 + j - 1)
                dve.tensor_copy(xsT[:, p, :], bank[0][:, 0:P]).then_inc(S("xsT_copied"), 1)

            def hidden(j):
                e = expert(dve, m, j)
                dve.wait_ge(S("h_ps"), n0 + j + 1)
                bias = b1r[:, bass.ds(e, 1), :].rearrange("p a f -> p (a f)")
                if m.kind == "gelu":
                    if due(n0 + j):
                        dve.wait_ge(S("h_ready"), n0 + j)
                    dve.tensor_tensor(hb[:, :], bank[1], bias, ALU.add).then_inc(S("hb_ready"), 1)
                else:
                    if due(n0 + j):
                        dve.wait_ge(S("hT_ps"), n0 + j)
                    dve.tensor_tensor(hs[:, :], bank[1], bias, ALU.add).then_inc(S("h_ready"), 1)

            def outputs(j, p):
                e = expert(dve, m, j)
                bias = b2r[:, m.layer // 2, bass.ds(e, 1), :].rearrange("p a d -> p (a d)")
                dve.wait_ge(S("y_ps"), n0 + j + 1)
                if m.kind == "gelu":
                    if due(j - 1):
                        dve.wait_ge(S("combined"), j - 1)
                    dve.tensor_scalar(oh[:, p, :], tokf, idxf[:, bass.ds(j, 1)], rv[:, bass.ds(j, 1)],
                                      ALU.is_equal, ALU.mult)
                    dve.tensor_tensor(ys[:, p, :], bank[3][:, 0:D], bias, ALU.add).then_inc(S("y_ready"), 1)
                else:
                    if due(m.stored(j, p)):
                        dve.wait_ge(S(f"y_st{p}"), m.stored(j, p))
                    dve.tensor_tensor(ys[:, p, :], bank[3][:, 0:D], bias, ALU.add).then_inc(S("y_ready"), 1)

            def stage(j, p):
                e = expert(dve, m, j)
                dve.wait_ge(S("h_ps"), n0 + j - 1)
                dve.tensor_copy(W1s[:, p, :], W1[3][:, bass.ds(e * F, F)]).then_inc(S("w1_staged"), 1)

            def step(j, p, ok):
                if m.kind == "silu":
                    if ok(1):
                        stage(j + 1, 1 - p)
                        copy_xsT(j + 1, 1 - p)
                    return
                if ok(-1):
                    copy_hT(j - 1)
                if ok(1):
                    copy_xsT(j + 1, 1 - p)
                if ok(0):
                    hidden(j)
                if ok(-1):
                    outputs(j - 1, 1 - p)

            steps(dve, m.nb, -1, m.nb + 1, step)

        def sp_blocks(sp, m):
            n0 = m.before

            def load(j, p):
                if due(n0 + j - 1):
                    sp.wait_ge(S("xsT_ps"), n0 + j - 1)
                sp.dma_start(xs[:, p, :], xs_d[bass.ds(j * P, P), :]).then_inc(S(f"xs_ld{p}"), 16)

            def store(j, p):
                sp.wait_ge(S("y_ready"), n0 + j + 1)
                sp.dma_start(ys_d[bass.ds(j * P, P), :], ys[:, p, :]).then_inc(S(f"y_st{p}"), 16)

            def step(j, p, ok):
                if ok(0):
                    load(j, p)
                if ok(-4):
                    store(j - 4, p)

            sp.wait_ge(S("scattered"), 16 * B * (m.route + 1))
            for j in range(4):
                step(j, j % 2, lambda d, j=j: 0 <= j + d < m.nb)
            pairs = (m.nb - 4) // 2
            with sp.Fori(0, pairs) as t:
                for p in range(2):
                    step(4 + 2 * t + p, p, lambda d: True)
            for j in range(4 + 2 * pairs, m.nb + 4):
                step(j, j % 2, lambda d, j=j: 0 <= j + d < m.nb)

        def pe_logits(pe, k, router, E, tiles=range(B)):
            for b in tiles:
                if b % 4 == 0:
                    pe.wait_ge(S("xnT_copied"), 2 * k.xt + b // 4 + 1)
                ins = pe.matmul(bank[4][:, E * b:E * b + E], xnT[:, P * b:P * b + P], router, start=True, stop=True)
            if b == B - 1:
                ins.then_inc(S("logits"), 1)

        def pe_counts(pe, k, E):
            pe.wait_ge(S("onehot"), k.route + 1)
            pe.matmul(bank[5][:, 0:B * E], tri[:, :], ohb[:, 0:B * E], start=True, stop=False)
            for b in range(B - 1):
                n = B - 1 - b
                pe.matmul(bank[5][:, E * b + E:B * E].rearrange("p (b e) -> p b e", b=n), onesb[:, :],
                          ohb[:, E * b:E * b + E].unsqueeze(1).to_broadcast([P, n, E]),
                          start=False, stop=b == B - 2)
            for b in range(B):
                ins = pe.matmul(bank[5][:, 256:256 + E], onesb[:, :], ohb[:, E * b:E * b + E],
                                start=b == 0, stop=b == B - 1)
            ins.then_inc(S("counts"), 1)

        def dve_softmax(dve, link, k, E, bias=None):
            v = lambda t: t[:, 0:B * E].rearrange("p (b e) -> p b e", b=B)
            dve.wait_ge(S("logits"), k.logits + 1)
            if bias is None:
                link(dve, dve.tensor_copy(lg[:, 0:B * E], bank[4][:, 0:B * E]))
            else:
                link(dve, dve.tensor_tensor(v(lg), v(bank[4]), bias.unsqueeze(1).to_broadcast([P, B, E]), ALU.add))
            link(dve, dve.tensor_reduce(r1[:, :].unsqueeze(2), v(lg), AX.X, ALU.max))
            dve.tensor_tensor(v(lg), v(lg), r1[:, :].unsqueeze(2).to_broadcast([P, B, E]), ALU.subtract
                              ).then_inc(S("logits_shifted"), 1)
            dve.wait_ge(S("logits_exp"), k.exps + 1)
            link(dve, dve.tensor_reduce(r1[:, :].unsqueeze(2), v(lt), AX.X, ALU.add))
            link(dve, dve.reciprocal(r1[:, :], r1[:, :]))
            return dve.tensor_tensor(v(lt), v(lt), r1[:, :].unsqueeze(2).to_broadcast([P, B, E]), ALU.mult)

        def act_softmax(act, k, E):
            act.wait_ge(S("logits_shifted"), k.exps + 1)
            act.activation(lt[:, 0:B * E], lg[:, 0:B * E], ACT.Exp).then_inc(S("logits_exp"), 1)
            if E == E16:
                act.activation(spare[:, :], half[:, 0:1], ACT.Silu)

        def dve_route(dve, link, k, E, nb, src):
            v = lambda t: t[:, 0:B * E].rearrange("p (b e) -> p b e", b=B)
            wide = lambda t: t[:, :].unsqueeze(2).to_broadcast([P, B, E])
            over = lambda t: t[:, 0:E].unsqueeze(1).to_broadcast([P, B, E])
            link(dve, dve.tensor_reduce(wtop[:, :].unsqueeze(2), v(src), AX.X, ALU.max))
            link(dve, dve.tensor_tensor(v(lg), v(src), wide(wtop), ALU.is_equal))
            link(dve, dve.tensor_tensor(v(lg), v(lg), over(erev), ALU.mult))
            link(dve, dve.tensor_reduce(r1[:, :].unsqueeze(2), v(lg), AX.X, ALU.max))
            dve.tensor_tensor(v(ohb), v(lg), wide(r1), ALU.is_equal).then_inc(S("onehot"), 1)
            dve.wait_ge(S("counts"), k.route + 1)
            link(dve, dve.tensor_scalar(ci[:, 0:E], bank[5][:, 256:256 + E], float(P - 1), None, ALU.add))
            link(dve, dve.tensor_scalar(ci[:, 0:E], ci[:, 0:E], 7, None, ALU.arith_shift_right))
            link(dve, dve.tensor_copy(c1[:, 0:E], ci[:, 0:E]))
            link(dve, dve.tensor_tensor_scan(c2[:, 0:E], ones[:, 0:E], c1[:, 0:E], 0.0, ALU.mult, ALU.add))
            link(dve, dve.tensor_tensor(c1[:, 0:E], c2[:, 0:E], c1[:, 0:E], ALU.subtract))
            link(dve, dve.scalar_tensor_tensor(v(lg), over(c1), float(P), v(bank[5]), ALU.mult, ALU.add))
            link(dve, dve.tensor_tensor(v(lg), v(lg), v(ohb), ALU.mult))
            link(dve, dve.tensor_reduce(slotf[:, :].unsqueeze(2), v(lg), AX.X, ALU.add))
            dve.tensor_copy(slot[:, :], slotf[:, :]).then_inc(S("slots"), 1)
            link(dve, dve.tensor_tensor(jcmp[:, 0:nb, 0:E], c2[0:1, 0:E].unsqueeze(1).to_broadcast([1, nb, E]),
                                        jrow[:, 0:nb].unsqueeze(2).to_broadcast([1, nb, E]), ALU.is_le))
            link(dve, dve.tensor_reduce(bef[:, 0:nb].unsqueeze(2), jcmp[:, 0:nb, 0:E], AX.X, ALU.add))
            dve.tensor_scalar(be[:, 0:nb], bef[:, 0:nb], float(E - 1), None, ALU.min).then_inc(S("block_experts"), 1)

        def pool_scatter(pool, k, src):
            pool.wait_ge(S("slots_cleared"), 16)
            pool.wait_ge(S("slots"), k.route + 1)
            for b in range(B):
                pool.indirect_dma_start(xs_d[:, :], bass.IndirectOffsetOnAxis(slot[:, b:b + 1], 0), src[:, b, :], None
                                        ).then_inc(S("scattered"), 16)

        def pool_gather(pool, m):
            for p in range(2):
                pool.wait_ge(S(f"y_st{p}"), m.all_stored(p))
            for b in range(B):
                pool.indirect_dma_start(yg[:, b, :], None, ys_d[0:P * m.nb, :], bass.IndirectOffsetOnAxis(slot[:, b:b + 1], 0)
                                        ).then_inc(S(f"back{b // 4}"), 16)

        def pe_choice(pe):
            pe_xnT(pe, 1, "xn_ready", B)
            pe_logits(pe, M0, rw[:, 0, :], E8)
            pe.wait_ge(S("probs"), 1)
            for b in range(B):
                ins = pe.transpose(bank[6 + b // 4][0:E8, P * (b % 4):P * (b % 4) + P], lt[:, E8 * b:E8 * b + E8],
                                   ident[:, :])
            ins.then_inc(S("probsT"), 1)
            pe.wait_ge(S("chosen"), 1)
            for n in range(2):
                ins = pe.transpose(bank[4][:, E8 * n:E8 * n + E8], top[:, n, :], ident[0:E8, 0:E8])
            ins.then_inc(S("chosenT"), 1)
            pe.wait_ge(S("sums_clear"), 1)
            pe_blocks(pe, M0)

        def dve_choice(dve, link):
            dve_softmax(dve, link, M0, E8, bs8[:, :]).then_inc(S("probs"), 1)
            dve.wait_ge(S("probsT"), 1)
            link(dve, dve.tensor_copy(work[:, :], psum[0:E8, 6:8, :].rearrange("p a n -> p (a n)")))
            for r in range(CAP // 8):
                t = slice(8 * r, 8 * r + 8)
                link(dve, dve.max(top[:, 0, t], work[:, :]))
                dve.max_index(topi[:, t], top[:, 0, t], work[:, :])
                link(dve, dve.match_replace(work[:, :], top[:, 0, t], work[:, :], -1.0))
            dve.tensor_copy(top[:, 1, :], topi[:, :]).then_inc(S("chosen"), 1)
            dve.wait_ge(S("chosenT"), 1)
            dve.tensor_copy(rv[:, :], bank[4][:, 0:E8])
            dve.tensor_copy(idxf[:, :], bank[4][:, E8:2 * E8])
            dve.tensor_copy(idx[:, :], bank[4][:, E8:2 * E8]).then_inc(S("indices"), 1)
            dve.memset(psum[:, 6:8, :], 0.0).then_inc(S("sums_clear"), 1)
            dve.wait_ge(S("indices"), 1)
            dve.wait_ge(S("tokens_numbered"), 1)
            dve_blocks(dve, link, M0)
            dve.wait_ge(S("combined"), M0.nb)
            xf = x[:, :, :].rearrange("p b d -> p (b d)")
            dve.tensor_tensor(xf, xf, psum[:, 6:8, :].rearrange("p a n -> p (a n)"), ALU.add
                              ).then_inc(S("x_combined"), 1)
            dve.wait_ge(S("x_combined"), 1)

        def pool_choice(pool, link):
            def gather(j):
                p = j % 2
                if due(j - 1):
                    pool.wait_ge(S("xsT_ps"), j - 1)
                pool.indirect_dma_start(xs[:, p, :], None, xn_d[:, :], bass.IndirectOffsetOnAxis(idx[:, j:j + 1], 0)
                                        ).then_inc(S(f"gathered{p}"), 16)

            link(pool, pool.iota(toki, [[1, B * P]], 0, 0))
            pool.tensor_copy(tokf, toki).then_inc(S("tokens_numbered"), 1)
            pool.wait_ge(S("indices"), 1)
            pool.wait_ge(S("xn_stored"), 16)
            for j in range(B):
                gather(j)

        def dve_quantised_weights(dve, link):
            v = wqr[:, :, :].rearrange("p n (k i) -> p (n k) i", i=32)
            wide = lambda t: t[:, :].unsqueeze(2).to_broadcast([P, 36, 32])
            flat = wqr[:, :, :].rearrange("p n k -> p (n k)")
            dve.wait_ge(S("ld_wqr"), 48)
            link(dve, dve.tensor_reduce(wsc[:, :].unsqueeze(2), v, AX.X, ALU.max, apply_absolute_value=True))
            link(dve, dve.tensor_scalar(wsc[:, :], wsc[:, :], 1.0 / WMAX, TINY, ALU.mult, ALU.max))
            link(dve, dve.reciprocal(wrc[:, :], wsc[:, :]))
            link(dve, dve.tensor_tensor(v, v, wide(wrc), ALU.mult))
            link(dve, dve.tensor_scalar(flat, flat, WMAX, -WMAX - 1.0, ALU.min, ALU.max))
            link(dve, dve.tensor_scalar(flat, flat, MAGIC, MAGIC, ALU.add, ALU.subtract))
            dve.tensor_tensor(v, v, wide(wsc), ALU.mult).then_inc(S("wq4"), 1)

        def pe_quantised_weights(pe):
            pe.wait_ge(S("wq4"), 1)
            for n in range(3):
                for t in range(QC):
                    ins = pe.transpose(bank[5 + n][:, P * t:P * t + P], wqr[:, n, P * t:P * t + P], ident[:, :])
                ins.then_inc(S("wq4T_ps"), 1)

        def act_quantised_weights(act):
            for n in range(3):
                act.wait_ge(S("wq4T_ps"), n + 1)
                act.activation(wqT[:, n, :], bank[5 + n][:, 0:QF], ACT.Copy).then_inc(S("wq4T"), 1)

        def dve_scale(dve, link, k, unit=None):
            dve.wait_ge(S("row_max_ps"), k + 1)
            dve.tensor_reduce(qrow[:, :], bank[7][0:1, 0:P], AX.X, ALU.max).then_inc(S("max_one"), 1)
            dve.wait_ge(S("max_all_ps"), k + 1)
            if unit is None:
                link(dve, dve.tensor_scalar(am[:, 6:7], bank[7][:, P:P + 1], 1.0, None, ALU.mult))
            else:
                link(dve, dve.tensor_scalar(am[:, 6:7], bank[7][:, P:P + 1], unit, None, ALU.mult))
            dst = qs[:, k, :] if k < 3 else qo[:, k - 3, :]
            link(dve, dve.tensor_scalar(dst[:, 0:1], am[:, 6:7], 1.0 / QMAX, TINY, ALU.mult, ALU.max))
            link(dve, dve.reciprocal(dst[:, 1:2], dst[:, 0:1]))
            if unit is not None:
                link(dve, dve.tensor_scalar(dst[:, 1:2], dst[:, 1:2], unit, None, ALU.mult))
            return dst

        def pe_scale(pe, k):
            pe.wait_ge(S("row_max"), k + 1)
            pe.transpose(bank[7][0:1, 0:P], am[:, 6:7], ident[:, :]).then_inc(S("row_max_ps"), 1)
            pe.wait_ge(S("max_one"), k + 1)
            pe.matmul(bank[7][:, P:P + 1], ones[0:1, :], qrow[:, :], start=True, stop=True
                      ).then_inc(S("max_all_ps"), 1)

        def dve_row_max(dve, t):
            dve.tensor_reduce(am[:, 6:7], t, AX.X, ALU.max, apply_absolute_value=True).then_inc(S("row_max"), 1)

        def to_integers(eng, link, t, r):
            link(eng, eng.tensor_scalar(t, t, r, QMAX, ALU.mult, ALU.min))
            link(eng, eng.tensor_scalar(t, t, -QMAX - 1.0, MAGIC, ALU.max, ALU.add))

        def dve_quantised(dve, link):
            flat = xn[:, :, :].rearrange("p b d -> p (b d)")
            dve.wait_ge(S("xn_ready"), 32)
            dve_row_max(dve, flat)
            q = dve_scale(dve, link, 0)
            to_integers(dve, link, flat, q[:, 1:2])
            dve.tensor_scalar(flat, flat, MAGIC, q[:, 0:1], ALU.subtract, ALU.mult).then_inc(S("xq_ready"), 1)
            for which, t in enumerate((QG, QU)):
                for n in range(6):
                    dve.wait_ge(S("gu_copied"), 6 * which + n + 1)
                    piece = t.rearrange("p (t n) -> p t n", t=QC)[:, n % 3, 512 * (n // 3):512 * (n // 3) + 512]
                    last = dve.tensor_reduce(am[:, n:n + 1], piece, AX.X, ALU.max, apply_absolute_value=True)
                link(dve, last)
                dve.tensor_reduce(am[:, 6:7], am[:, 0:6], AX.X, ALU.max).then_inc(S("row_max"), 1)
                q = dve_scale(dve, link, 1 + which)
                if which == 0:
                    to_integers(dve, link, QG, q[:, 1:2])
                    dve.tensor_scalar(QG, QG, MAGIC, q[:, 0:1], ALU.subtract, ALU.mult).then_inc(S("gate_q"), 1)
                else:
                    to_integers(dve, link, QU, q[:, 1:2])
                    link(dve, dve.tensor_scalar(QU, QU, MAGIC, q[:, 0:1], ALU.subtract, ALU.mult))
            dve.wait_ge(S("sigmoid"), 1)
            link(dve, dve.tensor_scalar(QV, QV, 65536.0, MAGIC, ALU.mult, ALU.add))
            link(dve, dve.tensor_scalar(QV, QV, MAGIC, MAGIC + 65535.0, ALU.max, ALU.min))
            link(dve, dve.scalar_tensor_tensor(QV, QV, MAGIC, QG, ALU.subtract, ALU.mult))
            dve_row_max(dve, QV)
            q = dve_scale(dve, link, 3, 2.0 ** -16)
            to_integers(dve, link, QV, q[:, 1:2])
            link(dve, dve.scalar_tensor_tensor(QV, QV, MAGIC, QU, ALU.subtract, ALU.mult))
            dve_row_max(dve, QV)
            q = dve_scale(dve, link, 4, q[:, 0:1])
            to_integers(dve, link, QV, q[:, 1:2])
            dve.tensor_scalar(QV, QV, MAGIC, q[:, 0:1], ALU.subtract, ALU.mult).then_inc(S("o_q"), 1)
            for n in range(2):
                dve.wait_ge(S("down_ps"), n + 1)
                xv = x[:, 4 * n:4 * n + 4, :].rearrange("p b d -> p (b d)")
                dve.tensor_tensor(xv, xv, bank[n], ALU.add).then_inc(S("x_quantised"), 1)
            dve.wait_ge(S("x_quantised"), 2)

        def act_quantised(act):
            for which, t in enumerate((QG, QU)):
                for n in range(6):
                    act.wait_ge(S("gu_ps"), 6 * which + n + 1)
                    piece = t.rearrange("p (t n) -> p t n", t=QC)[:, n % 3, 512 * (n // 3):512 * (n // 3) + 512]
                    act.activation(piece, bank[n], ACT.Copy).then_inc(S("gu_copied"), 1)
            act.wait_ge(S("gate_q"), 1)
            act.activation(QV, QG, ACT.Sigmoid).then_inc(S("sigmoid"), 1)
            for e in range(E8):
                act.wait_ge(S("b1_folded_ps"), e + 1)
                act.activation(b1r[:, e, :], bank[6], ACT.Copy).then_inc(S("b1_folded"), 1)
                w = W1[2][:, F * e:F * e + F]
                act.activation(w, w, ACT.Copy, scale=lnT[:, 0, e:e + 1]).then_inc(S("w1_folded"), 1)

        def pe_quantised(pe):
            pe_scale(pe, 0)
            pe.wait_ge(S("xq_ready"), 1)
            pe_xnT(pe, 3, "xn_ready", 3 * B)
            pe.wait_ge(S("wq4T"), 3)
            pe.wait_ge(S("xnT_copied"), 8)
            for which in range(2):
                for n in range(6):
                    if which:
                        pe.wait_ge(S("gu_copied"), n + 1)
                    pe.matmul(bank[n], wqT[:, which, P * (n % 3):P * (n % 3) + P],
                              xnT[:, 512 * (n // 3):512 * (n // 3) + 512], start=True, stop=True
                              ).then_inc(S("gu_ps"), 1)
            pe.wait_ge(S("ld_e2"), 16 * (1 + FC))
            pe.wait_ge(S("ld_b2"), 32)

            def fold(experts):
                for e in experts:
                    if e:
                        pe.wait_ge(S("b1_folded"), e)
                    w = slice(F * e, F * e + F)
                    pe.matmul(bank[6], lnT[:, 1, e:e + 1].to_broadcast([P, P]), W1[2][:, w], start=True, stop=False)
                    pe.matmul(bank[6], ident[0:E8, e:e + 1].to_broadcast([E8, P]), b8[:, :], start=False, stop=True
                              ).then_inc(S("b1_folded_ps"), 1)

            pe_scale(pe, 1)
            fold((0,))
            pe_scale(pe, 2)
            fold((1, 2))
            pe_scale(pe, 3)
            fold((3,))
            pe_scale(pe, 4)
            fold((4,))
            pe.wait_ge(S("o_q"), 1)
            for b in range(B):
                for c in range(QC):
                    ins = pe.matmul(bank[b // 4][:, P * (b % 4):P * (b % 4) + P],
                                    QV[:, B * P * c + P * b:B * P * c + P * b + P], wqT[:, 2, P * c:P * c + P],
                                    start=c == 0, stop=c == QC - 1)
                if b % 4 == 3:
                    ins.then_inc(S("down_ps"), 1)
            fold((5, 6, 7))

        def dve_top(dve, link):
            dve.wait_ge(S("xn_ready"), 6 * B)
            dve_layernorm(dve, link, 6, xn, xn2)
            dve.wait_ge(S("logits"), M1.logits + 1)
            link(dve, dve.tensor_copy(lt[:, 0:B * E8], bank[4][:, 0:B * E8]))
            dve_route(dve, link, M1, E8, NB8, lt)
            dve.wait_ge(S("ld_b2"), 32)
            dve_blocks(dve, link, M1)
            link(dve, dve.tensor_tensor(x[:, :, :], x[:, :, :], xn[:, :, :], ALU.add))
            for n in range(2):
                dve.wait_ge(S(f"back{n}"), 64)
                h = slice(4 * n, 4 * n + 4)
                last = dve.tensor_tensor(x[:, h, :], x[:, h, :], yg[:, h, :], ALU.add)
            link(dve, last)

        def pe_top(pe):
            pe_xnT(pe, 5, "xn_ready", 5 * B)
            pe_logits(pe, M1, rw[:, 1, :], E8)
            pe_counts(pe, M1, E8)
            pe.wait_ge(S("block_experts"), 1)
            pe.wait_ge(S("w1_folded"), E8)
            pe_blocks(pe, M1)

        def pool_top(pool, link):
            pool_rstd(pool, link, 6)
            pool.wait_ge(S("xn_ready"), 7 * B)
            pool_scatter(pool, M1, xn2)
            pool_gather(pool, M1)

        def dve_chain(dve, link, k):
            dve_softmax(dve, link, k, E16).then_inc(S("chain_probs"), 1)
            if due(k.exps):
                dve.wait_ge(S("chain_probs"), k.exps)
            dve_route(dve, link, k, E16, NB16, lt)
            dve.wait_ge(S("block_experts"), k.route + 1)
            if k is MC[0]:
                dve.wait_ge(S("ld_e3"), 16 * (1 + FC))
            dve_blocks(dve, link, k)
            for n in range(2):
                dve.wait_ge(S(f"back{n}"), 64 * (k.route + 1))
                h = slice(4 * n, 4 * n + 4)
                w = wtop[:, h].unsqueeze(2).to_broadcast([P, 4, D])
                if k is not MC[-1]:
                    dve.tensor_tensor(xn[:, h, :], yg[:, h, :], w, ALU.mult).then_inc(S("chain_ready"), 1)
                else:
                    link(dve, dve.tensor_tensor(yg[:, h, :], yg[:, h, :], w, ALU.mult))
                    dve.tensor_tensor(x[:, h, :], x[:, h, :], yg[:, h, :], ALU.add).then_inc(S("x_final"), 1)

        def pe_chain(pe, k, i):
            if i == 0:
                pe.wait_ge(S("ld_rw16"), 16)
                pe_xnT(pe, k.xt, "xn_ready", 8 * B)
                pe_logits(pe, k, rw16[:, i, :], E16)
            else:
                for n in range(2):
                    half_tiles = range(4 * n, 4 * n + 4)
                    pe.wait_ge(S("chain_ready"), 2 * (i - 1) + n + 1)
                    for b in half_tiles:
                        ins = pe.transpose(bank[n][:, P * (b % 4):P * (b % 4) + P], xn[:, b, :], ident[:, :])
                    ins.then_inc(S("xnT_ps"), 1)
                    pe_logits(pe, k, rw16[:, i, :], E16, half_tiles)
            pe_counts(pe, k, E16)
            pe.wait_ge(S("block_experts"), k.route + 1)
            if i == 0:
                pe.wait_ge(S("ld_e3"), 16 * (1 + FC))
            pe_blocks(pe, k)

        block = ctx.enter_context(nc.Block())

        @block.sync
        def _(sp):
            row = lambda ap: ap.rearrange("(a n) -> a n", a=1)
            hdk = lambda ap: ap.rearrange("h d k -> d h k")
            hd = lambda ap: ap.rearrange("(a h d) -> a h d", a=1, d=DH)
            sp.dma_start(craw, a["ctx_1024"].rearrange("b p d -> p b d")).then_inc(S("ld_ctx"), 16)
            for n, k in enumerate(["L0_xattn_Wq", "L0_xattn_Wk"]):
                sp.dma_start(wraw[:, n, :], a[k]).then_inc(S("ld_w0"), 16)
            sp.wait_ge(S("brow_clear"), 2)
            for n, ap in ((2, hd(a["L2_xattn_bq"])), (6, hd(a["L2_xattn_bkv"][0:D])),
                          (3, a["L3_xattn_bq"].rearrange("h (a d) -> a h d", a=1)),
                          (7, a["L3_xattn_bk"].rearrange("h (a d) -> a h d", a=1))):
                sp.dma_start(brow[0:1, n, :, 0:DH], ap).then_inc(S("ld_brow"), 16)
            sp.dma_start(x[:, :, :], a["x"].rearrange("b p d -> p b d")).then_inc(S("ld_x"), 16)
            sp.dma_start(wv[:, 0, :], a["L0_xattn_Wv"]).then_inc(S("ld_wv0"), 16)
            sp.dma_start(wo[:, 0, :], a["L0_xattn_Wo"]).then_inc(S("ld_wv0"), 16)
            for n, k in enumerate(["w_gate", "w_up"]):
                sp.dma_start(wqr[:, n, :].rearrange("p (t i) -> p t i", t=QC),
                             a["L1_ffn_" + k].rearrange("(t p) i -> p t i", p=P)).then_inc(S("ld_wqr"), 16)
            sp.dma_start(wqr[:, 2, :], a["L1_ffn_w_down"]).then_inc(S("ld_wqr"), 16)
            for n, k in enumerate(["W_q", "W_k", "W_v", "W_proj"]):
                sp.dma_start(wraw[:, 6 + n, :], a["L1_xattn_" + k]).then_inc(S("ld_wt"), 16)
            for n, k in enumerate(["ln_g", "ln_b", "centroids"]):
                sp.dma_start(e8w[:, n, :], a["L2_ffn_" + k]).then_inc(S("ld_e8w"), 16)
            sp.dma_start(wraw[:, 2, :], a["L2_xattn_Wq"]).then_inc(S("ld_w"), 16)
            sp.dma_start(wraw[:, 3, :], a["L2_xattn_Wkv"][:, 0:D]).then_inc(S("ld_w"), 16)
            for n, k in ((4, "L3_xattn_Wq"), (5, "L3_xattn_Wk")):
                sp.dma_start(wraw[:, n, :].rearrange("p (h k) -> p h k", h=H), hdk(a[k])).then_inc(S("ld_w"), 16)
            sp.dma_start(mask8[:, :, :], a["mask_Bx1xSxS2_bk0"].rearrange("b a q k -> q (a b) k")
                         ).then_inc(S("ld_mask"), 16)
            k = "L0_ffn_"
            sp.dma_start(b2r[:, 0, :, :].rearrange("p e d -> p (e d)"),
                         a[k + "b2"].rearrange("e (a d) -> a (e d)", a=1).to_broadcast([P, E8 * D])
                         ).then_inc(S("ld_b0"), 16)
            sp.dma_start(b1r[:, :, :].rearrange("p e f -> p (e f)"),
                         a[k + "b1"].rearrange("e (a f) -> a (e f)", a=1).to_broadcast([P, E8 * F])
                         ).then_inc(S("ld_b0"), 16)
            sp.dma_start(rw[:, 0, :], a[k + "Ws"]).then_inc(S("ld_b0"), 16)
            sp.dma_start(bs8[:, :], row(a[k + "bs"]).to_broadcast([P, E8])).then_inc(S("ld_b0"), 16)
            sp.dma_start(wv[:, 2, :], a["L2_xattn_Wkv"][:, D:2 * D]).then_inc(S("ld_wv"), 16)
            sp.dma_start(wv[:, 3, :].rearrange("p (h k) -> p h k", h=H), hdk(a["L3_xattn_Wv"])).then_inc(S("ld_wv"), 16)
            sp.dma_start(wo[:, 2, :], a["L2_xattn_Wo"]).then_inc(S("ld_wv"), 16)
            sp.dma_start(wo[:, 3, :], a["L3_xattn_Wo"]).then_inc(S("ld_wv"), 16)
            sp.dma_start(bv[:, 0, :], row(a["L2_xattn_bkv"][D:2 * D]).to_broadcast([P, D])).then_inc(S("ld_bo"), 16)
            sp.dma_start(bv[:, 1, :], a["L3_xattn_bv"].rearrange("h (a d) -> a (h d)", a=1).to_broadcast([P, D])
                         ).then_inc(S("ld_bo"), 16)
            for n, k in enumerate(["L1_xattn_b_proj", "L2_xattn_bo", "L3_xattn_bo"]):
                sp.dma_start(bo[:, n, :], row(a[k]).to_broadcast([P, D])).then_inc(S("ld_bo"), 16)
            sp.dma_start(b2r[:, 1, :, :].rearrange("p e d -> p (e d)"),
                         a["L2_ffn_b2"].rearrange("e (a d) -> a (e d)", a=1).to_broadcast([P, E8 * D])
                         ).then_inc(S("ld_b2"), 16)
            sp.dma_start(b8[:, :], a["L2_ffn_b1"]).then_inc(S("ld_b2"), 16)
            sp.dma_start(rw16[:, :, :], a["L3_ffn_routers"].rearrange("n d e -> d n e")).then_inc(S("ld_rw16"), 16)
            sp.wait_ge(S("zero"), 1)
            sp.dma_start(xs_d.rearrange("(j p) d -> p j d", p=P), hT[:, 0:D].unsqueeze(1).to_broadcast([P, NB16, D])
                         ).then_inc(S("slots_cleared"), 16)
            sp.wait_ge(S("xn_ready"), 2 * B)
            sp.dma_start(xn_d.rearrange("(b p) d -> p b d", p=P), xn[:, :, :]).then_inc(S("xn_stored"), 16)
            sp.wait_ge(S("y_ready"), M0.nb)
            sp.dma_start(W1[3].rearrange("p (e f) -> p e f", e=E16), a["L3_ffn_W1"].rearrange("e d f -> d e f")
                         ).then_inc(S("ld_e3"), 16)
            sp_blocks(sp, M1)
            for c in range(FC):
                sp.dma_start(W2[3].rearrange("p (e c d) -> p e c d", e=E16, c=FC)[:, :, c, :],
                             a["L3_ffn_W2"][:, P * c:P * c + P, :].rearrange("e p d -> p e d")).then_inc(S("ld_e3"), 16)
            for k in MC:
                sp_blocks(sp, k)
            for n in range(2):
                sp.wait_ge(S("x_final"), n + 1)
                sp.dma_start(out[4 * n:4 * n + 4, :, :].rearrange("b p d -> p b d"), x[:, 4 * n:4 * n + 4, :]
                             ).then_inc(S("st_out"), 16)
            sp.wait_ge(S("st_out"), 32)

        @block.gpsimd
        def _(pool):
            link = Link(S("pool_step"))
            pool.memset(brow[:, :, :, :], 0.0).then_inc(S("brow_clear"), 1)
            pool.wait_ge(S("brow_clear"), 1)
            pool.memset(brow[:, 4:8, :, DH:DH + 1], 1.0).then_inc(S("brow_clear"), 1)
            pool.memset(ident[:, :], 0.0)
            pool.memset(tri[:, :], 1.0)
            pool.memset(ones[:, :], 1.0)
            pool.memset(onesb[:, :], 1.0)
            pool.memset(hmask[:, :], 1.0)
            pool.memset(half[:, :], -0.5)
            pool.memset(sel[:, :, :], 0.0)
            pool.memset(hT[:, :], 0.0).then_inc(S("zero"), 1)
            pool.memset(Mp[:, :, :], 0.0)
            pool.memset(Va[:, :, :, DH:DH + 1], 1.0)
            pool.memset(wq[:, :, :, :], 0.0)
            link(pool, pool.memset(wk[:, :, :, :], 0.0))
            pool.iota(iot[:, :], [[1, 24]], 0, 0)
            link(pool, pool.affine_select(out=tri[:, :], in_=tri[:, :], compare_op=ALU.is_gt, fill=0.0, base=0,
                                          pattern=[[1, P]], channel_multiplier=-1))
            link(pool, pool.affine_select(out=hmask[:, :], in_=hmask[:, :], compare_op=ALU.is_ge, fill=0.0, base=0,
                                          pattern=[[-ROWS, HC]], channel_multiplier=1))
            link(pool, pool.affine_select(out=ident[:, :], in_=ident[:, :], compare_op=ALU.not_equal, fill=1.0,
                                          base=0, pattern=[[-1, P]], channel_multiplier=1))
            link(pool, pool.affine_select(out=sel[:, :, :], in_=sel[:, :, :], compare_op=ALU.not_equal, fill=1.0,
                                          base=0, pattern=[[-32, 4], [-1, DH + 1]], channel_multiplier=1))
            link(pool, pool.affine_select(out=hmask[:, :], in_=hmask[:, :], compare_op=ALU.is_ge, fill=0.0,
                                          base=ROWS - 1, pattern=[[ROWS, HC]], channel_multiplier=-1))
            pool.tensor_copy(identb[:, :], ident[:, :]).then_inc(S("consts"), 1)
            pool.tensor_scalar(erev[:, :], iot[:, 0:E16], -1.0, float(E16), ALU.mult, ALU.add)
            link(pool, pool.tensor_copy(jrow[:, :], iot[0:1, :]))
            for name, layer, n in PAD:
                if n == 0:
                    pool.wait_ge(S("ld_w0"), 32)
                if n == 2:
                    pool.wait_ge(S("ld_w"), 16 * (len(PAD) - 2))
                dst = (wq if name == "wq" else wk)[:, layer, :, 0:DH]
                pool.tensor_copy(dst, wraw[:, n, :].rearrange("p (h d) -> p h d", h=H)).then_inc(S("w_pad"), 1)
                if n == 1:
                    pool_rstd(pool, link, XL[0])
            for L in range(4):
                if L > 0:
                    pool_rstd(pool, link, XL[L])
                pool_attention(pool, L)
                pool_rstd(pool, link, XL[L] + 1)
                if L == 0:
                    pool_choice(pool, link)
                if L == 2:
                    pool_top(pool, link)
                if L == 3:
                    for k in MC:
                        pool_scatter(pool, k, xn)
                        pool_gather(pool, k)

        @block.scalar
        def _(act):
            for n in range(2):
                act.wait_ge(S("ctx_ps"), n + 1)
                act.activation(ctxT[:, 512 * n:512 * n + 512], bank[n], ACT.Copy).then_inc(S("ctx_copied"), 1)
            act.wait_ge(S("bcol_ps"), 1)
            act.activation(bcol[:, :, :].rearrange("p n c -> p (n c)"), bank[2][:, 0:16], ACT.Copy
                           ).then_inc(S("bcol_copied"), 1)
            act.wait_ge(S("bcol_copied"), 1)
            for L in (0, 2):
                k = f"L{L}_ffn_"
                act.dma_start(W1[L].rearrange("p (e f) -> p e f", e=E8), a[k + "W1"].rearrange("e d f -> d e f")
                              ).then_inc(S(f"ld_e{L}"), 16)
                for c in range(FC):
                    act.dma_start(W2[L].rearrange("p (e c d) -> p e c d", e=E8, c=FC)[:, :, c, :],
                                  a[k + "W2"][:, P * c:P * c + P, :].rearrange("e p d -> p e d")
                                  ).then_inc(S(f"ld_e{L}"), 16)
            for L in range(4):
                act_attention(act, L)
                act_xnT(act, 2 * L + 1)
                if L == 0:
                    act_softmax(act, M0, E8)
                    act_blocks(act, M0)
                if L == 1:
                    act_quantised(act)
                if L == 3:
                    for k in MC:
                        if k is not MC[0]:
                            act_xnT(act, k.xt)
                        act_softmax(act, k, E16)
                        act_blocks(act, k)

        @block.vector
        def _(dve):
            link = Link(S("dve_step"))
            dve.wait_ge(S("ld_x"), 16)
            for L in range(4):
                dve_layernorm(dve, link, XL[L], x, xn)
                if L == 0:
                    dve_quantised_weights(dve, link)
                dve_attention(dve, link, L)
                dve_layernorm(dve, link, XL[L] + 1, x, xn)
                if L == 0:
                    dve.wait_ge(S("ld_b0"), 64)
                    dve_choice(dve, link)
                if L == 1:
                    dve_quantised(dve, link)
                if L == 2:
                    dve_top(dve, link)
                if L == 3:
                    for k in MC:
                        dve_chain(dve, link, k)

        @block.tensor
        def _(pe):
            pe.wait_ge(S("consts"), 1)
            pe.wait_ge(S("ld_ctx"), 16)
            for b in range(B):
                ins = pe.transpose(bank[b // 4][:, P * (b % 4):P * (b % 4) + P], craw[:, b, :], ident[:, :])
                if b % 4 == 3:
                    ins.then_inc(S("ctx_ps"), 1)
            pe.wait_ge(S("ld_brow"), 64)
            pe.wait_ge(S("brow_clear"), 2)
            for n in range(8):
                for c in range(2):
                    ins = pe.matmul(bank[2][:, 2 * n + c:2 * n + c + 1],
                                    brow[0:1, n, HC * c:HC * c + HC, :].rearrange("p h r -> p (h r)"),
                                    ones[0:1, 0:1], start=True, stop=True)
            ins.then_inc(S("bcol_ps"), 1)
            pe.wait_ge(S("ctx_copied"), 2)
            pe.wait_ge(S("w_pad"), 2)
            pe.wait_ge(S("ld_wv0"), 32)
            pe.wait_ge(S("bcol_copied"), 1)
            for L in range(4):
                pe_attention(pe, L)
                if L == 0:
                    pe.wait_ge(S("ld_b0"), 64)
                    pe.wait_ge(S("ld_e0"), 16 * (1 + FC))
                    pe_choice(pe)
                if L == 1:
                    pe_quantised(pe)
                if L == 2:
                    pe_top(pe)
                if L == 3:
                    for i, k in enumerate(MC):
                        pe_chain(pe, k, i)


XL = [0, 2, 4, 7]
XT = [0, 2, 4, 6]
XR = [0, 16, 32, 56]

_OUT = (B, P, D)


def kernel(**inputs):
    import numpy as _np
    import concourse.bacc as _bacc
    from concourse.bass_utils import run_bass_kernel_spmd as _run

    nc = _bacc.Bacc("TRN2", target_bir_lowering=False, num_devices=1)
    arrays, args = {}, {}
    for name in inputs:
        v = _np.ascontiguousarray(inputs[name])
        arrays[f"in_{name}"] = v
        args[name] = nc.dram_tensor(f"in_{name}", v.shape, mybir.dt.from_np(v.dtype), kind="ExternalInput").ap()
    out = nc.dram_tensor("out_0", _OUT, F32, kind="ExternalOutput").ap()
    build(nc, args, out)
    r = _run(nc, [arrays], core_ids=[0])
    return r.results[0]["out_0"]
```
